# Optimizing a Trainium2 kernel written in Bass

```python
import numpy as np
import jax
import jax.numpy as jnp

def _softmax(x, axis=-1):
    return jax.nn.softmax(x, axis=axis)

def _gelu(x):
    return jax.nn.gelu(x, approximate=True)

def _silu(x):
    return jax.nn.silu(x)

def _sigmoid(x):
    return jax.nn.sigmoid(x)

def _layernorm(x, axis=-1, eps=1e-05):
    m = jnp.mean(x, axis=axis, keepdims=True)
    v = jnp.var(x, axis=axis, keepdims=True)
    return (x - m) / jnp.sqrt(v + eps)

def _scatter_add(tgt, idx, src, axis=0):
    return tgt.at[idx].add(src)

def _segment_sum(src, seg, n):
    return jax.ops.segment_sum(src, seg, n)
kernel_name = 'mk_adj_ffn_d1_adj_r2_488191'

def setup_inputs(seed: int=0):
    np.random.seed(seed)
    _w = jnp.asarray

    def _rec_inputs():
        import jax
        import jax.numpy as jnp
        _gk = jax.random.key(seed)
        x = -0.0005207 + 1.001 * jax.random.normal(jax.random.fold_in(_gk, 1), (8192, 128), jnp.float32)
        _a = jax.random.bernoulli(jax.random.fold_in(_gk, 2), 0.000488281, (8192, 8192))
        _a = jnp.logical_or(_a, jnp.eye(8192, dtype=bool))
        _af = _a.astype(jnp.float32)
        _af = _af / jnp.maximum(_af.sum(-1, keepdims=True), 1.0)
        adj = _af
        return (x, adj)
    x, adj = _rec_inputs()

    def _L0_gnn_setup():
        import jax, jax.numpy as jnp
        import numpy as np
        N = 4096
        IN_DIM = 128
        OUT_DIM = 128
        key = jax.random.key(seed)
        k1, k2, k3 = jax.random.split(key, 3)
        features = jax.random.normal(k1, (N, IN_DIM), dtype=jnp.float32)
        A = jax.random.uniform(k2, (N, N), dtype=jnp.float32)
        A = A / jnp.sum(A, axis=-1, keepdims=True)
        weight = jax.random.normal(k3, (IN_DIM * 2, OUT_DIM), dtype=jnp.float32) * np.sqrt(6.0 / (IN_DIM * 2 + OUT_DIM))
        bias = jnp.zeros((OUT_DIM,), dtype=jnp.float32)
        return {'features': features, 'A': A, 'weight': weight, 'bias': bias}
    _L0_gnn_all = _L0_gnn_setup()
    _L0_gnn_in = {k: v for k, v in _L0_gnn_all.items() if k in ('weight', 'bias')}
    del _L0_gnn_all

    def _L0_ffn_setup():
        import jax, jax.numpy as jnp
        import numpy as np
        C = 128
        HID = 512
        E = 8
        TEMP = 1.0
        key = jax.random.key(seed)
        ks = jax.random.split(key, 7)
        x = jax.random.normal(ks[0], (8, 8192, C), dtype=jnp.float32)
        W1 = jax.random.normal(ks[1], (C, HID), dtype=jnp.float32) * 0.02
        b1 = jnp.zeros((HID,), dtype=jnp.float32)
        Wg = jax.random.normal(ks[2], (HID, E), dtype=jnp.float32) * 0.02
        bg = jnp.zeros((E,), dtype=jnp.float32)
        Wd = jax.random.normal(ks[3], (E, HID, C), dtype=jnp.float32) * 0.02
        bd = jnp.zeros((E, C), dtype=jnp.float32)
        return {'x': x, 'W1': W1, 'b1': b1, 'Wg': Wg, 'bg': bg, 'Wd': Wd, 'bd': bd}
    _L0_ffn_all = _L0_ffn_setup()
    _L0_ffn_in = {k: v for k, v in _L0_ffn_all.items() if k in ('W1', 'b1', 'Wg', 'bg', 'Wd', 'bd')}
    del _L0_ffn_all
    return {'x': x, 'adj': adj, 'L0_gnn_weight': _L0_gnn_in['weight'], 'L0_gnn_bias': _L0_gnn_in['bias'], 'L0_ffn_W1': _L0_ffn_in['W1'], 'L0_ffn_b1': _L0_ffn_in['b1'], 'L0_ffn_Wg': _L0_ffn_in['Wg'], 'L0_ffn_bg': _L0_ffn_in['bg'], 'L0_ffn_Wd': _L0_ffn_in['Wd'], 'L0_ffn_bd': _L0_ffn_in['bd']}

def reference(x, adj, L0_gnn_weight, L0_gnn_bias, L0_ffn_W1, L0_ffn_b1, L0_ffn_Wg, L0_ffn_bg, L0_ffn_Wd, L0_ffn_bd):
    import jax
    import jax.numpy as jnp

    def _L0_gnn_ref(features, A, weight, bias):
        import jax, jax.numpy as jnp
        import numpy as np
        N = 4096
        IN_DIM = 128
        OUT_DIM = 128
        agg_feats = jnp.matmul(A, features)
        cat_feats = jnp.concatenate([features, agg_feats], axis=-1)
        out = jnp.einsum('nd,df->nf', cat_feats, weight)
        return jax.nn.relu(out + bias)

    def _L0_ffn_ref(x, W1, b1, Wg, bg, Wd, bd):
        import jax, jax.numpy as jnp
        import numpy as np
        C = 128
        HID = 512
        E = 8
        TEMP = 1.0
        orig_shape = x.shape
        xf = x.reshape(-1, orig_shape[-1])
        H = jax.nn.gelu(xf @ W1 + b1, approximate=False)
        probs = jax.nn.softmax((H @ Wg + bg) / TEMP, axis=-1)
        assign = jnp.argmax(probs, axis=-1)
        out = jnp.zeros_like(xf)
        for e in range(Wd.shape[0]):
            y = H @ Wd[e] + bd[e]
            sel = (assign == e)[:, None]
            out = out + jnp.where(sel, probs[:, e:e + 1] * y, 0.0)
        return out.reshape(orig_shape)
    x = x + _L0_gnn_ref(_layernorm(x, axis=-1), adj, L0_gnn_weight, L0_gnn_bias)
    x = x + _L0_ffn_ref(_layernorm(x, axis=-1)[None], L0_ffn_W1, L0_ffn_b1, L0_ffn_Wg, L0_ffn_bg, L0_ffn_Wd, L0_ffn_bd)[0]
    return x

_drawn_inputs = setup_inputs


def setup_inputs(seed=0):
    import zlib

    import numpy as np

    out = dict(_drawn_inputs(seed))
    spreads = {'L0_gnn_bias': (0.0, 0.1),
     'L0_ffn_b1': (0.0, 0.8),
     'L0_ffn_bg': (0.0, 0.628),
     'L0_ffn_bd': (0.0, 0.8)}
    factors = {'L0_ffn_W1': 7.651, 'L0_ffn_Wg': 7.237, 'L0_ffn_Wd': 8.0}
    for name, (base, spread) in spreads.items():
        noise = np.random.default_rng([zlib.crc32(name.encode()), seed]).standard_normal(out[name].shape)
        drawn = base * np.exp(spread * noise) if base else spread * noise
        out[name] = jnp.asarray(drawn.astype(out[name].dtype))
    for name, factor in factors.items():
        out[name] = (out[name] * factor).astype(out[name].dtype)
    return out
```

```python
from contextlib import ExitStack

import concourse.bass as bass
from concourse import mybir

F32 = mybir.dt.float32
F32R = mybir.dt.float32r
BF16 = mybir.dt.bfloat16
I32 = mybir.dt.int32
U32 = mybir.dt.uint32
ALU = mybir.AluOpType
ACT = mybir.ActivationFunctionType
AX_X = mybir.AxisListType.X

P = 128
N = 8192
D = 128
HID = 512
E = 8
BT = 4
BN = BT * P
NB = N // BN
KH = HID // P
G = 4
NC = N // P // G
RAW = 4
HC = 2
GH = G // HC
NH = NC * HC
HL = 4
XS = 4
REGION = N + P
ROW = D + 4
DUMMY = E * REGION
MAXT = N // P + E
assert MAXT % 12 == 0
PAIRS = MAXT // 2
EPS = 1e-5
RING = 6

C_ID, C_TRI, C_ONE = 0, P, 2 * P
C_IOTA = 3 * P
C_BASE = C_IOTA + E
C_HALF = C_BASE + E + 1
C_E = C_HALF + BT
C_P = C_E + BT * E
C_J = C_P + 1
C_ROW0 = C_J + MAXT
C_LEN = C_ROW0 + P


def bass_gnn_moe_kernel(nc, x, adj, w12, gnn_b, w1, b1, wg, bg, wd, bd, consts, tokens, out):
    with ExitStack() as ctx:
        def sb(name, shape, dt=F32, stack=ctx):
            return stack.enter_context(nc.sbuf_tensor(name, shape, dt))

        def sem(name):
            return ctx.enter_context(nc.semaphore(name))

        buckets = nc.dram_tensor("buckets", [DUMMY + P, ROW], F32, kind="Internal").ap()

        ps = ctx.enter_context(nc.psum_tensor("ps", [P, 8, 512], F32))
        AGG, TB, HB, GB, ZB = 0, 2, 3, 5, 6
        H2B, T2B, YB = 0, 4, 6

        cst = sb("cst", [P, C_LEN])
        tri = sb("tri", [P, P], BF16)
        ones = sb("ones", [P, P], BF16)
        w1h = sb("w1h", [P, HID], F32R)
        w1l = sb("w1l", [P, HID], F32R)
        b1c = sb("b1c", [P, KH])
        run = sb("run", [P, E + 1])
        ident = cst[:, C_ID:C_ID + P]

        one = ExitStack()
        raw = sb("raw", [P, RAW, HC, GH * BN], stack=one)
        zh = sb("zh", [P, N], F32R, one)
        zl = sb("zl", [P, N], F32R, one)
        hi = sb("hi", [P, HL, GH * BN], F32R, one)
        lo = sb("lo", [P, HL, GH * BN], F32R, one)
        u = sb("u", [P, N], F32, one)
        xg = sb("xg", [P, XS, BN], F32, one)
        hid = sb("hid", [P, KH, BN], F32, one)
        w1raw = hid[:, 0, :]
        turned = sb("turned", [P, BN], F32, one)
        pre = sb("pre", [P, BN], F32, one)
        xn = sb("xn", [P, BT, D], F32, one)
        xh = sb("xh", [P, BN], F32R, one)
        xl = sb("xl", [P, BN], F32R, one)
        rows = sb("rows", [P, 2, BT, ROW], F32, one)
        padrows = sb("padrows", [P, ROW], F32, one)
        w12s = sb("w12s", [P, 2 * D], F32, one)
        wgs = sb("wgs", [P, KH, E], F32, one)
        gbb = sb("gbb", [P, D], F32, one)
        bgb = sb("bgb", [P, E], F32, one)
        tok = sb("tok", [P, N // P], I32, one)
        st = sb("st", [P, BT, 6], F32, one)
        ms = sb("ms", [P, BT], F32, one)
        md = sb("md", [P, BT], F32, one)
        vs = sb("vs", [P, BT], F32, one)
        ve = sb("ve", [P, BT], F32, one)
        rs = sb("rs", [P, BT], F32, one)
        nm = sb("nm", [P, BT], F32, one)
        lg = sb("lg", [P, BT, E], F32, one)
        mx = sb("mx", [P, BT], F32, one)
        df = sb("df", [P, BT, E], F32, one)
        ex = sb("ex", [P, BT, E], F32, one)
        cand = sb("cand", [P, BT, E], F32, one)
        first = sb("first", [P, BT], F32, one)
        oh = sb("oh", [P, BT, E], BF16, one)
        sm = sb("sm", [P, BT], F32, one)
        place = sb("place", [P, BT, E], F32, one)
        slotf = sb("slotf", [P, BT], F32, one)
        slot = sb("slot", [P, 2, BT], U32, one)
        padslot = sb("padslot", [P, E + 1], I32, one)
        one.close()

        two = ctx
        wdraw = sb("wdraw", [P, KH * E * D], F32, two)
        rows2 = sb("rows2", [P, RING, 2, ROW], F32, two)
        tail0 = sb("tail0", [P, 2, 2 * D], F32, two)
        nt = sb("nt", [P, E], F32, two)
        cnt = sb("cnt", [P, E], I32, two)
        cnt2 = sb("cnt2", [P, E], I32, two)
        end = sb("end", [P, E], F32, two)
        past = sb("past", [P, MAXT, E], F32, two)
        pastn = sb("pastn", [P, MAXT, E], F32, two)
        ej = sb("ej", [P, MAXT], F32, two)
        sj = sb("sj", [P, MAXT], F32, two)
        used = sb("used", [P, MAXT], F32, two)
        rj = sb("rj", [P, MAXT], F32, two)
        tab = sb("tab", [P, 2, MAXT], I32, two)
        fill = sb("fill", [P, (RAW * G * BN - KH * E * D - RING * 2 * ROW - 4 * D - 4 * E
                               - 2 * MAXT * E - 6 * MAXT)], F32, two)
        wdh = sb("wdh", [P, KH, E * D], F32R, two)
        wdl = sb("wdl", [P, KH, E * D], F32R, two)
        bdb = sb("bdb", [P, E * D], F32, two)
        xh2 = sb("xh2", [P, 2, 2 * P], F32R, two)
        xl2 = sb("xl2", [P, 2, 2 * P], F32R, two)
        hid2 = sb("hid2", [P, KH, 2 * P], F32, two)
        hh = sb("hh", [P, 2, KH, 2 * P], F32R, two)
        hl = sb("hl", [P, 2, KH, 2 * P], F32R, two)
        ids = sb("ids", [P, 2, 2], U32, two)
        bdh = sb("bdh", [P, E * D], F32R, two)
        bdl = sb("bdl", [P, E * D], F32R, two)
        pick0 = sb("pick0", [P, P], F32R, two)
        o2 = sb("o2", [P, 2, 2, D], F32, two)

        raw_in = [sem(f"raw_in{s}") for s in range(RAW)]
        xg_in = [sem(f"xg_in{s}") for s in range(XS)]
        cst_in, w_in = sem("cst_in"), sem("w_in")
        cast_done, w1h_done, w1l_done, pad_done = sem("cast_done"), sem("w1h_done"), sem("w1l_done"), sem("pad_done")
        hi_done, lo_done, part_done = sem("hi_done"), sem("lo_done"), sem("part_done")
        bn_done, parts_done, var_done = sem("bn_done"), sem("parts_done"), sem("var_done")
        ve_done, rs_done = sem("ve_done"), sem("rs_done")
        nm_done, xn_done, xnt_done = sem("nm_done"), sem("xn_done"), sem("xnt_done")
        turned_done, zu_done, zh_done, zl_done = sem("turned_done"), sem("zu_done"), sem("zh_done"), sem("zl_done")
        agt_done, ag_turned, pre_done, x2_done = sem("agt_done"), sem("ag_turned"), sem("pre_done"), sem("x2_done")
        xh_done, xl_done, h_done, gelu_done = sem("xh_done"), sem("xl_done"), sem("h_done"), sem("gelu_done")
        gate_done, lg_done, mx_done, df_done = sem("gate_done"), sem("lg_done"), sem("mx_done"), sem("df_done")
        ex_done, less_done, cand_done, first_done = sem("ex_done"), sem("less_done"), sem("cand_done"), sem("first_done")
        oh_done, sum_done, prob_done, count_done = sem("oh_done"), sem("sum_done"), sem("prob_done"), sem("count_done")
        at_done, pick_done, slotf_done, slot_done = sem("at_done"), sem("pick_done"), sem("slotf_done"), sem("slot_done")
        run_done, scattered = sem("run_done"), sem("scattered")
        padslot_done, padded, step_done, tab_done = sem("padslot_done"), sem("padded"), sem("step_done"), sem("tab_done")
        wd_in, bd_in, wdh_done, wdl_done = sem("wd_in"), sem("bd_in"), sem("wdh_done"), sem("wdl_done")
        rows_in = [sem(f"rows_in{s}") for s in range(RING)]
        n2_done, t2_done, xh2_done, xl2_done = sem("n2_done"), sem("t2_done"), sem("xh2_done"), sem("xl2_done")
        h2_done, gelu2_done, hh_done, hl_done = sem("h2_done"), sem("gelu2_done"), sem("hh_done"), sem("hl_done")
        y_done, out_done = sem("y_done"), sem("out_done")
        bdh_done, bdl_done, pick_in = sem("bdh_done"), sem("bdl_done"), sem("pick_in")
        o_done = [sem(f"o_done{s}") for s in range(RING)]
        stored = [sem("stored0"), sem("stored1")]

        def ln_index(q):
            return q + NC

        block = ctx.enter_context(nc.Block())

        @block.sync
        def _(sp):
            def load_x(slot_, g, nth):
                sp.dma_start(xg[:, slot_, :], x[bass.ds(g * P, P), :]).then_inc(xg_in[slot_], 16)

            def load_chunk(b, c):
                if not (isinstance(b, int) and b == 0 and c < RAW):
                    sp.wait_ge(lo_done, b * NH + (c - RAW + 1) * HC)
                sp.dma_start(raw[:, c % RAW, :, :].rearrange("p h n -> p (h n)"), adj[bass.ds((b * NC + c) * P, P), :]).then_inc(raw_in[c % RAW], 16)

            sp.dma_start(cst[:], consts).then_inc(cst_in, 16)
            for g in range(XS):
                load_x(g, g, 0)
            sp.dma_start(w12s[:], w12).then_inc(w_in, 16)
            sp.dma_start(gbb[:], gnn_b.partition_broadcast(P)).then_inc(w_in, 16)
            sp.dma_start(bgb[:], bg.partition_broadcast(P)).then_inc(w_in, 16)
            sp.dma_start(w1raw, w1).then_inc(w_in, 16)
            sp.dma_start(wgs[:].rearrange("p k e -> p (k e)"), wg).then_inc(w_in, 16)
            sp.dma_start(b1c[:], b1).then_inc(w_in, 16)
            sp.dma_start(tok[:], tokens).then_inc(w_in, 16)
            for c in range(NC):
                load_chunk(0, c)
                g = c + XS
                if g < NC:
                    sp.wait_ge(xn_done, g - XS + 1)
                    load_x(g % XS, g, g // XS)

            def block_loads(b, s):
                for c in range(NC):
                    load_chunk(b, c)
                    if c == 0:
                        if isinstance(b, int):
                            sp.wait_ge(xn_done, NC)
                            if b >= 3:
                                sp.wait_ge(x2_done, b - 2)
                        else:
                            sp.wait_ge(x2_done, b - 2)
                        load_x(s, b - 1, 0)

            block_loads(1, 0)
            block_loads(2, 1)
            with sp.Fori(1, NB // 2 - 1) as i:
                block_loads(i * 2 + 1, 0)
                block_loads(i * 2 + 2, 1)
            block_loads(NB - 1, 0)
            sp.wait_ge(x2_done, NB - 2)
            load_x(1, NB - 1, 0)
            sp.wait_ge(lo_done, NB * NH)
            sp.dma_start(wdraw[:], wd).then_inc(wd_in, 16)
            sp.wait_ge(part_done, NB * NH)
            sp.dma_start(bdb[:], bd.partition_broadcast(P)).then_inc(bd_in, 16)

            def load_rows(k, nth, i):
                for t in range(2):
                    r = sp.value_load(tab[0:1, 0, bass.ds(i * 2 + t, 1)], min_val=0, max_val=DUMMY)
                    sp.dma_start(rows2[:, k, t, :], buckets[bass.ds(r, P), :]).then_inc(rows_in[k], 16)

            sp.wait_ge(pad_done, 1)
            sp.wait_ge(padslot_done, 1)
            for e in range(E + 1):
                r = sp.value_load(padslot[0:1, e:e + 1], min_val=0, max_val=DUMMY)
                sp.dma_start(buckets[bass.ds(r, P), :], padrows[:]).then_inc(padded, 16)

            sp.wait_ge(tab_done, 1)
            sp.wait_ge(scattered, 16 * BT * NB)
            sp.wait_ge(padded, 16 * (E + 1))
            for k in range(RING):
                load_rows(k, 0, k)
            with sp.Fori(1, PAIRS // RING) as i:
                for k in range(RING):
                    sp.wait_ge(o_done[k], i)
                    load_rows(k, 0, i * RING + k)

        @block.scalar
        def _(act):
            def split_hi(b, c):
                act.wait_ge(raw_in[c % RAW], (b * (NC // RAW) + c // RAW + 1) * 16)
                for h in range(HC):
                    j = c * HC + h
                    if not (isinstance(b, int) and b == 0 and j < HL):
                        act.wait_ge(part_done, b * NH + (j - HL + 1))
                    act.copy(hi[:, j % HL, :], raw[:, c % RAW, h, :]).then_inc(hi_done, 1)

            act.wait_ge(w_in, 16 * 7)
            act.copy(w1h[:], w1raw).then_inc(w1h_done, 1)

            def turned_copy(g):
                act.wait_ge(xnt_done, g + 1)
                if g >= 1:
                    act.wait_ge(zu_done, g)
                act.copy(turned[:], ps[:, TB, :]).then_inc(turned_done, 1)

            def z_hi(g):
                act.wait_ge(zu_done, g + 1)
                act.copy(zh[:, g * BN:(g + 1) * BN].rearrange("p (t d) -> p t d", t=BT),
                         ps[:, ZB:ZB + 2, :].rearrange("p a (b d) -> p (a b) d", b=4)[:, 1::2, :]).then_inc(zh_done, 1)

            turned_copy(0)
            turned_copy(1)
            for c in range(NC):
                z_hi(c)
                if c + 2 < NC:
                    turned_copy(c + 2)
                split_hi(0, c)

            def aggregate_copy(q, s):
                act.wait_ge(part_done, q * NH + NH)
                act.copy(turned[:], ps[:, AGG + s, :]).then_inc(agt_done, 1)

            def ln_hi(q):
                act.wait_ge(xnt_done, ln_index(q) + 1)
                act.copy(xh[:], ps[:, TB, :]).then_inc(xh_done, 1)

            def gelu(q, h):
                act.wait_ge(h_done, q * KH + (h + 1))
                act.activation(hid[:, h, :], ps[:, HB + h % 2, :], ACT.Gelu, bias=b1c[:, h:h + 1]).then_inc(gelu_done, 1)

            def behind(q, s, c):
                if c == 1:
                    aggregate_copy(q, s)
                if c == 9:
                    ln_hi(q)
                if c == 12:
                    gelu(q, 0)
                    gelu(q, 1)
                if c == 14:
                    gelu(q, 2)
                    gelu(q, 3)

            def body(b, s):
                for c in range(NC):
                    behind(b - 1, 1 - s, c)
                    split_hi(b, c)

            body(1, 1)
            with act.Fori(1, NB // 2) as i:
                body(i * 2, 0)
                body(i * 2 + 1, 1)
            for c in range(NC):
                behind(NB - 1, (NB - 1) % 2, c)

            act.wait_ge(wd_in, 16)
            act.wait_ge(part_done, NB * NH)
            act.copy(wdh[:].rearrange("p k n -> p (k n)"), wdraw[:]).then_inc(wdh_done, 1)

            act.wait_ge(bd_in, 16)
            act.copy(bdh[:], bdb[:]).then_inc(bdh_done, 1)
            act.copy(pick0[:], cst[:, C_ROW0:C_ROW0 + P]).then_inc(pick_in, 1)

            def ln_hi2(i, s):
                act.wait_ge(t2_done, i + 1)
                act.copy(xh2[:, s, :], ps[:, T2B + s, 0:2 * P]).then_inc(xh2_done, 1)

            def hidden_hi(i, s):
                act.wait_ge(h2_done, i + 1)
                if not (isinstance(i, int) and i == 0):
                    act.wait_ge(hl_done, i)
                for h in range(KH):
                    act.activation(hid2[:, h, :], ps[:, H2B + 2 * s + h // 2, (h % 2) * 2 * P:(h % 2 + 1) * 2 * P],
                                   ACT.Gelu, bias=b1c[:, h:h + 1]).then_inc(gelu2_done, 1)
                act.wait_ge(gelu2_done, i * KH + KH)
                if not (isinstance(i, int) and i < 2):
                    act.wait_ge(y_done, i - 1)
                act.copy(hh[:, s, :, :], hid2[:]).then_inc(hh_done, 1)

            ln_hi2(0, 0)
            ln_hi2(1, 1)
            hidden_hi(0, 0)
            ln_hi2(2, 0)
            hidden_hi(1, 1)
            with act.Fori(1, PAIRS // 2 - 1) as i:
                ln_hi2(i * 2 + 1, 1)
                hidden_hi(i * 2, 0)
                ln_hi2(i * 2 + 2, 0)
                hidden_hi(i * 2 + 1, 1)
            ln_hi2(PAIRS - 1, 1)
            hidden_hi(PAIRS - 2, 0)
            hidden_hi(PAIRS - 1, 1)

        @block.vector
        def _(dve):
            dve.wait_ge(cst_in, 16)
            nc.vector.tensor_copy(tri[:], cst[:, C_TRI:C_TRI + P])
            nc.vector.tensor_copy(ones[:], cst[:, C_ONE:C_ONE + P])
            nc.vector.tensor_copy(run[:], cst[:, C_BASE:C_BASE + E + 1]).then_inc(cast_done, 1)

            def split_lo(b, c):
                for h in range(HC):
                    j = c * HC + h
                    dve.wait_ge(hi_done, b * NH + (j + 1))
                    nc.vector.tensor_tensor(lo[:, j % HL, :], raw[:, c % RAW, h, :], hi[:, j % HL, :].bitcast(F32),
                                            ALU.subtract).then_inc(lo_done, 1)

            def ln_stats(n, tile):
                for t in range(BT):
                    last = nc.vector.bn_stats(st[:, t, :], tile(t))
                last.then_inc(bn_done, 1)
                dve.wait_ge(bn_done, n + 1)
                nc.vector.tensor_tensor(ms[:], st[:, :, 1], st[:, :, 4], ALU.add)
                nc.vector.tensor_tensor(md[:], st[:, :, 1], st[:, :, 4], ALU.subtract)
                nc.vector.tensor_tensor(vs[:], st[:, :, 2], st[:, :, 5], ALU.add).then_inc(parts_done, 1)
                dve.wait_ge(parts_done, n + 1)
                nc.vector.scalar_tensor_tensor(out=md[:], in0=md[:], scalar=0.25, in1=md[:],
                                               op0=ALU.mult, op1=ALU.mult)
                nc.vector.tensor_scalar(vs[:], vs[:], 1.0 / D, EPS, ALU.mult, ALU.add).then_inc(var_done, 1)
                dve.wait_ge(var_done, n + 1)
                nc.vector.tensor_tensor(ve[:], md[:], vs[:], ALU.add).then_inc(ve_done, 1)

            def ln_apply(n, tile):
                dve.wait_ge(rs_done, n + 1)
                nc.vector.scalar_tensor_tensor(out=nm[:], in0=ms[:], scalar=-0.5, in1=rs[:],
                                               op0=ALU.mult, op1=ALU.mult).then_inc(nm_done, 1)
                dve.wait_ge(nm_done, n + 1)
                if not (isinstance(n, int) and n == 0):
                    dve.wait_ge(xnt_done, n)
                for t in range(BT):
                    last = nc.vector.tensor_scalar(xn[:, t, :], tile(t), rs[:, t:t + 1], nm[:, t:t + 1],
                                                   ALU.mult, ALU.add)
                last.then_inc(xn_done, 1)

            def x_tile(g):
                return lambda t: xg[:, g % XS, t * D:(t + 1) * D]

            def start_stats(g):
                dve.wait_ge(xg_in[g % XS], 16 * (g // XS + 1))
                ln_stats(g, x_tile(g))

            def z_lo(g):
                dve.wait_ge(zh_done, g + 1)
                zu = ps[:, ZB:ZB + 2, :].rearrange("p a (b d) -> p (a b) d", b=4)
                nc.vector.tensor_tensor(u[:, g * BN:(g + 1) * BN].rearrange("p (t d) -> p t d", t=BT), zu[:, 0::2, :],
                                        gbb[:].unsqueeze(1).to_broadcast([P, BT, D]), ALU.add)
                sl = slice(g * BN, (g + 1) * BN)
                nc.vector.tensor_tensor(zl[:, sl].rearrange("p (t d) -> p t d", t=BT), zu[:, 1::2, :],
                                        zh[:, sl].bitcast(F32).rearrange("p (t d) -> p t d", t=BT),
                                        ALU.subtract).then_inc(zl_done, 1)

            dve.wait_ge(w1h_done, 1)
            nc.vector.tensor_tensor(w1l[:], w1raw, w1h[:].bitcast(F32), ALU.subtract).then_inc(w1l_done, 1)
            start_stats(0)
            ln_apply(0, x_tile(0))
            for g in range(1, 3):
                start_stats(g)
                ln_apply(g, x_tile(g))
            start_stats(3)
            for c in range(NC):
                z_lo(c)
                split_lo(0, c)
                if c + 3 < NC:
                    ln_apply(c + 3, x_tile(c + 3))
                if c + 4 < NC:
                    start_stats(c + 4)

            def residual(q, s):
                dve.wait_ge(ag_turned, q + 1)
                nc.vector.tensor_tensor(pre[:], ps[:, TB, :], u[:, bass.ds(q * BN, BN)], ALU.add).then_inc(pre_done, 1)
                if isinstance(q, int):
                    dve.wait_ge(xg_in[s], 16 * (NC // XS + q // 2 + 1))
                dve.wait_ge(pre_done, q + 1)
                if not (isinstance(q, int) and q < 2):
                    dve.wait_ge(scattered, (q - 1) * (16 * BT))
                nc.vector.scalar_tensor_tensor(out=rows[:, s, :, 0:D], in0=pre[:].rearrange("p (t d) -> p t d", t=BT),
                                               scalar=0.0, in1=xg[:, s, :].rearrange("p (t d) -> p t d", t=BT),
                                               op0=ALU.max, op1=ALU.add).then_inc(x2_done, 1)

            def x2_tile(s):
                return lambda t: rows[:, s, t, 0:D]

            def ln_lo(q, s):
                dve.wait_ge(xh_done, q + 1)
                nc.vector.tensor_tensor(xl[:], ps[:, TB, :], xh[:].bitcast(F32), ALU.subtract).then_inc(xl_done, 1)

            def row_scalars(q, s):
                nc.vector.tensor_copy(rows[:, s, :, D], rs[:])
                nc.vector.tensor_copy(rows[:, s, :, D + 1], nm[:])

            def behind(q, s, c, xcount):
                if c == 4:
                    dve.wait_ge(xg_in[s], xcount)
                    residual(q, s)
                if c == 5:
                    dve.wait_ge(x2_done, q + 1)
                    ln_stats(ln_index(q), x2_tile(s))
                if c == 7:
                    ln_apply(ln_index(q), x2_tile(s))
                    row_scalars(q, s)
                if c == 10:
                    ln_lo(q, s)

            def route(r, s, c):
                four = ps[:, GB, 0:BT * E].rearrange("p (t e) -> p t e", t=BT)
                iota = cst[:, C_IOTA:C_IOTA + E].unsqueeze(1).to_broadcast([P, BT, E])
                if c == 0:
                    dve.wait_ge(gate_done, r + 1)
                    nc.vector.tensor_tensor(lg[:], four, bgb[:].unsqueeze(1).to_broadcast([P, BT, E]),
                                            ALU.add).then_inc(lg_done, 1)
                if c == 1:
                    dve.wait_ge(lg_done, r + 1)
                    nc.vector.tensor_reduce(mx[:], lg[:], AX_X, ALU.max).then_inc(mx_done, 1)
                    dve.wait_ge(mx_done, r + 1)
                    nc.vector.tensor_tensor(df[:], lg[:], mx[:].unsqueeze(2).to_broadcast([P, BT, E]),
                                            ALU.subtract).then_inc(df_done, 1)
                if c == 2:
                    dve.wait_ge(df_done, r + 1)
                    nc.vector.tensor_scalar(cand[:], df[:], 0.0, float(E), ALU.is_lt, ALU.mult).then_inc(less_done, 1)
                    dve.wait_ge(less_done, r + 1)
                    nc.vector.tensor_tensor(cand[:], cand[:], iota, ALU.add).then_inc(cand_done, 1)
                    dve.wait_ge(cand_done, r + 1)
                    nc.vector.tensor_reduce(first[:], cand[:], AX_X, ALU.min).then_inc(first_done, 1)
                if c == 3:
                    dve.wait_ge(first_done, r + 1)
                    nc.vector.tensor_tensor(oh[:], iota, first[:].unsqueeze(2).to_broadcast([P, BT, E]),
                                            ALU.is_equal).then_inc(oh_done, 1)
                if c == 6:
                    dve.wait_ge(ex_done, r + 1)
                    nc.vector.tensor_reduce(sm[:], ex[:], AX_X, ALU.add).then_inc(sum_done, 1)
                    dve.wait_ge(sum_done, r + 1)
                    nc.vector.reciprocal(rows[:, s, :, D + 2], sm[:]).then_inc(prob_done, 1)
                if c == 8:
                    dve.wait_ge(count_done, r + 1)
                    nc.vector.tensor_tensor(place[:], four, run[:, 0:E].unsqueeze(1).to_broadcast([P, BT, E]),
                                            ALU.add).then_inc(at_done, 1)
                    nc.vector.tensor_copy(rows[:, s, :, D + 3].bitcast(I32), tok[:, bass.ds(r * BT, BT)])
                if c == 9:
                    dve.wait_ge(at_done, r + 1)
                    nc.vector.tensor_tensor(place[:], place[:], oh[:], ALU.mult).then_inc(pick_done, 1)
                    nc.vector.tensor_tensor(run[:, 0:E], run[:, 0:E], ps[:, GB, BT * E:(BT + 1) * E],
                                            ALU.add).then_inc(run_done, 1)
                    dve.wait_ge(pick_done, r + 1)
                    nc.vector.tensor_reduce(slotf[:], place[:], AX_X, ALU.add).then_inc(slotf_done, 1)
                    dve.wait_ge(slotf_done, r + 1)
                    nc.vector.tensor_copy(slot[:, s, :], slotf[:]).then_inc(slot_done, 1)

            def body(b, s, xcount, routed=True):
                for c in range(NC):
                    behind(b - 1, 1 - s, c, xcount)
                    if routed:
                        route(b - 2, s, c)
                    split_lo(b, c)

            starts = NC // XS
            body(1, 1, 16 * (starts + 1), routed=False)
            with dve.Fori(1, NB // 2) as i:
                body(i * 2, 0, (i + starts) * 16)
                body(i * 2 + 1, 1, (i + (starts + 1)) * 16)
            for c in range(NC):
                behind(NB - 1, 1, c, 16 * (starts + NB // 2))
                route(NB - 2, 0, c)
            for c in range(NC):
                route(NB - 1, 1, c)

            dve.wait_ge(run_done, NB)
            nc.vector.tensor_copy(padslot[:], run[:]).then_inc(padslot_done, 1)

            steps = [0]

            def then(ins):
                ins.then_inc(step_done, 1)
                steps[0] += 1
                dve.wait_ge(step_done, steps[0])

            dve.wait_ge(lo_done, NB * NH)
            then(nc.vector.tensor_tensor(nt[:], run[:, 0:E], cst[:, C_BASE:C_BASE + E], ALU.subtract))
            then(nc.vector.tensor_scalar(cnt[:], nt[:], float(P - 1), None, ALU.add))
            then(nc.vector.tensor_scalar(cnt2[:], cnt[:], 7, None, ALU.arith_shift_right))
            then(nc.vector.tensor_copy(nt[:], cnt2[:]))
            then(nc.vector.tensor_copy(end[:, 0:1], nt[:, 0:1]))
            for e in range(1, E):
                then(nc.vector.tensor_tensor(end[:, e:e + 1], end[:, e - 1:e], nt[:, e:e + 1], ALU.add))
            js = cst[:, C_J:C_J + MAXT]
            then(nc.vector.tensor_tensor(past[:], js.unsqueeze(2).to_broadcast([P, MAXT, E]),
                                         end[:].unsqueeze(1).to_broadcast([P, MAXT, E]), ALU.is_ge))
            nc.vector.tensor_reduce(ej[:], past[:], AX_X, ALU.add)
            then(nc.vector.tensor_tensor(pastn[:], past[:], nt[:].unsqueeze(1).to_broadcast([P, MAXT, E]), ALU.mult))
            then(nc.vector.tensor_reduce(sj[:], pastn[:], AX_X, ALU.add))
            nc.vector.tensor_scalar(used[:], ej[:], float(E), float(P), ALU.is_lt, ALU.mult)
            then(nc.vector.tensor_tensor(sj[:], js, sj[:], ALU.subtract))
            then(nc.vector.tensor_tensor(sj[:], sj[:], used[:], ALU.mult))
            then(nc.vector.scalar_tensor_tensor(out=rj[:], in0=ej[:], scalar=float(REGION), in1=sj[:],
                                                op0=ALU.mult, op1=ALU.add))
            nc.vector.tensor_copy(tab[:, 0, :], rj[:])
            then(nc.vector.tensor_scalar(ej[:], ej[:], float(E - 1), float(D), ALU.min, ALU.mult))
            nc.vector.tensor_copy(tab[:, 1, :], ej[:]).then_inc(tab_done, 1)

            dve.wait_ge(wdh_done, 1)
            nc.vector.tensor_tensor(wdl[:].rearrange("p k n -> p (k n)"), wdraw[:],
                                    wdh[:].bitcast(F32).rearrange("p k n -> p (k n)"), ALU.subtract).then_inc(wdl_done, 1)

            def normalise2(i, k, rcount):
                dve.wait_ge(rows_in[k], rcount)
                if not (isinstance(i, int) and i < 2):
                    dve.wait_ge(t2_done, i - 1)
                for t in range(2):
                    last = nc.vector.tensor_scalar(tail0[:, k % 2, t * D:(t + 1) * D], rows2[:, k, t, 0:D],
                                                   rows2[:, k, t, D:D + 1], rows2[:, k, t, D + 1:D + 2],
                                                   ALU.mult, ALU.add)
                last.then_inc(n2_done, 1)

            def ln_lo2(i, s):
                dve.wait_ge(xh2_done, i + 1)
                nc.vector.tensor_tensor(xl2[:, s, :], ps[:, T2B + s, 0:2 * P], xh2[:, s, :].bitcast(F32),
                                        ALU.subtract).then_inc(xl2_done, 1)

            def hidden_lo(i, s):
                dve.wait_ge(hh_done, i + 1)
                nc.vector.tensor_tensor(hl[:, s, :, :], hid2[:], hh[:, s, :, :].bitcast(F32),
                                        ALU.subtract).then_inc(hl_done, 1)

            def combine(i, k, ocount):
                s = k % 2
                dve.wait_ge(y_done, i + 1)
                if ocount is not None:
                    dve.wait_ge(stored[s], ocount)
                for t in range(2):
                    last = nc.vector.scalar_tensor_tensor(out=o2[:, s, t, :], in0=ps[:, YB + s, t * D:(t + 1) * D],
                                                          scalar=rows2[:, k, t, D + 2:D + 3],
                                                          in1=rows2[:, k, t, 0:D], op0=ALU.mult, op1=ALU.add)
                last.then_inc(out_done, 1)
                nc.vector.tensor_copy(ids[:, s, :], rows2[:, k, :, D + 3].bitcast(U32)).then_inc(o_done[k], 1)

            dve.wait_ge(bdh_done, 1)
            nc.vector.tensor_tensor(bdl[:], bdb[:], bdh[:].bitcast(F32), ALU.subtract).then_inc(bdl_done, 1)
            normalise2(0, 0, 32)
            normalise2(1, 1, 32)
            ln_lo2(0, 0)
            normalise2(2, 2, 32)
            ln_lo2(1, 1)
            hidden_lo(0, 0)

            def steps2(i, r, k, c_ok=True, n_ok=True, t_ok=True, h_ok=True, ocount=None):
                if t_ok:
                    ln_lo2(i + 2, k % 2)
                if n_ok:
                    normalise2(i + 3, (k + 3) % RING, (r + (k + 3) // RING + 1) * 32)
                if c_ok:
                    combine(i - 1, (k - 1) % RING, ocount)
                if h_ok:
                    hidden_lo(i + 1, (k + 1) % 2)

            def o_count(r, k):
                return r * (32 * RING // 2) + 32 * ((k - 3) // 2 + 1)

            for k in range(RING):
                steps2(k, 0, k, c_ok=k >= 1, ocount=o_count(0, k) if k >= 3 else None)
            with dve.Fori(1, PAIRS // RING - 1) as i:
                for k in range(RING):
                    steps2(i * RING + k, i, k, ocount=o_count(i, k))
            last_r = PAIRS // RING - 1
            for k in range(RING):
                i = last_r * RING + k
                steps2(i, last_r, k, n_ok=i + 3 < PAIRS, t_ok=i + 2 < PAIRS, h_ok=i + 1 < PAIRS,
                       ocount=o_count(last_r, k))
            combine(PAIRS - 1, RING - 1, o_count(last_r, RING))

        @block.gpsimd
        def _(pool):
            def rstd(n):
                pool.wait_ge(ve_done, n + 1)
                nc.gpsimd.tensor_tensor(rs[:], ve[:], cst[:, C_HALF:C_HALF + BT], ALU.pow).then_inc(rs_done, 1)

            def exps(r):
                pool.wait_ge(df_done, r + 1)
                nc.gpsimd.tensor_tensor(ex[:].rearrange("p t e -> p (t e)"), cst[:, C_E:C_E + BT * E],
                                        df[:].rearrange("p t e -> p (t e)"), ALU.pow).then_inc(ex_done, 1)

            def scatter(r, s):
                pool.wait_ge(cst_in, 16)
                pool.wait_ge(slot_done, r + 1)
                pool.wait_ge(prob_done, r + 1)
                for t in range(BT):
                    nc.gpsimd.indirect_dma_start(
                        out=buckets, out_offset=bass.IndirectOffsetOnAxis(ap=slot[:, s, t:t + 1], axis=0),
                        in_=rows[:, s, t, :], in_offset=None).then_inc(scattered, 16)

            nc.gpsimd.memset(padrows[:, 0:D + 3], 0.0)
            nc.gpsimd.memset(padrows[:, D + 3:ROW].bitcast(I32), N).then_inc(pad_done, 1)
            pool.wait_ge(cst_in, 16)
            for g in range(NC):
                rstd(g)
            rstd(ln_index(0))
            with pool.Fori(1, NB // 2) as i:
                for s in range(2):
                    r = i * 2 + (s - 2)
                    exps(r)
                    rstd(ln_index(r + 1))
                    scatter(r, s)
            exps(NB - 2)
            rstd(ln_index(NB - 1))
            scatter(NB - 2, 0)
            exps(NB - 1)
            scatter(NB - 1, 1)

            def store(r, k):
                pool.wait_ge(cst_in, 16)
                pool.wait_ge(o_done[k], r)
                for t in range(2):
                    nc.gpsimd.indirect_dma_start(
                        out=out, out_offset=bass.IndirectOffsetOnAxis(
                            ap=ids[:, k % 2, t:t + 1], axis=0),
                        in_=o2[:, k % 2, t, :], in_offset=None,
                        bounds_check=N - 1, oob_is_err=False).then_inc(stored[k % 2], 16)

            with pool.Fori(1, PAIRS // RING + 1) as i:
                for k in range(RING):
                    store(i, k)
            pool.wait_ge(stored[0], 16 * PAIRS)
            pool.wait_ge(stored[1], 16 * PAIRS)

        @block.tensor
        def _(pe):
            def split_product(dst, ah, al, bh, bl, start, stop):
                nc.tensor.matmul(dst, ah, bh, start=start, stop=False)
                nc.tensor.matmul(dst, ah, bl, start=False, stop=False)
                return nc.tensor.matmul(dst, al, bh, start=False, stop=stop)

            def chunk(b, s, c):
                for j in range(c * HC, (c + 1) * HC):
                    pe.wait_ge(lo_done, b * NH + (j + 1))
                    for g in range(GH):
                        k = j * GH + g
                        zs, ns = slice(k * P, (k + 1) * P), slice(g * BN, (g + 1) * BN)
                        last = split_product(ps[:, AGG + s, :], zh[:, zs], zl[:, zs], hi[:, j % HL, ns],
                                             lo[:, j % HL, ns], start=(k == 0), stop=(k == G * NC - 1))
                    last.then_inc(part_done, 1)

            def turn_norm(n):
                pe.wait_ge(xn_done, n + 1)
                for t in range(BT):
                    last = nc.tensor.transpose(ps[:, TB, t * P:(t + 1) * P], xn[:, t, :], ident)
                last.then_inc(xnt_done, 1)

            def z_and_u(g):
                pe.wait_ge(turned_done, g + 1)
                if g >= 1:
                    pe.wait_ge(zl_done, g)
                for t in range(BT):
                    last = nc.tensor.matmul(ps[:, ZB + t // 2, (t % 2) * 2 * D:(t % 2 + 1) * 2 * D],
                                            turned[:, t * P:(t + 1) * P], w12s[:], start=True, stop=True)
                last.then_inc(zu_done, 1)

            pe.wait_ge(cst_in, 16)
            pe.wait_ge(w_in, 16 * 7)
            turn_norm(0)
            pe.wait_ge(turned_done, 1)
            z_and_u(0)
            turn_norm(1)
            for c in range(NC):
                if c + 2 < NC:
                    pe.wait_ge(turned_done, c + 2)
                    turn_norm(c + 2)
                if c + 1 < NC:
                    z_and_u(c + 1)
                pe.wait_ge(zl_done, c + 1)
                chunk(0, 0, c)

            def behind(q, s, c):
                if c == 2:
                    pe.wait_ge(agt_done, q + 1)
                    for t in range(BT):
                        last = nc.tensor.transpose(ps[:, TB, t * P:(t + 1) * P], turned[:, t * P:(t + 1) * P], ident)
                    last.then_inc(ag_turned, 1)
                if c == 7:
                    turn_norm(ln_index(q))
                if c in (10, 12):
                    for h in range(c - 10, c - 8):
                        pe.wait_ge(xl_done, q + 1)
                        if c == 12:
                            pe.wait_ge(gelu_done, q * KH + (h - 1))
                        hs = slice(h * P, (h + 1) * P)
                        split_product(ps[:, HB + h % 2, :], w1h[:, hs], w1l[:, hs], xh[:], xl[:],
                                      start=True, stop=True).then_inc(h_done, 1)
                if c == 14:
                    pe.wait_ge(gelu_done, q * KH + KH)
                    for t in range(BT):
                        for h in range(KH):
                            last = nc.tensor.matmul(ps[:, GB, t * E:(t + 1) * E], hid[:, h, t * P:(t + 1) * P],
                                                    wgs[:, h, :], start=(h == 0), stop=(h == KH - 1))
                    last.then_inc(gate_done, 1)

            def count(r, c):
                if c == 5:
                    pe.wait_ge(oh_done, r + 1)
                    flat = oh[:].rearrange("p t e -> p (t e)")
                    nc.tensor.matmul(ps[:, GB, 0:BT * E], tri[:], flat, start=True, stop=False, skip_group_check=True)
                    for t in range(1, BT):
                        nc.tensor.matmul(ps[:, GB, t * E:BT * E], ones[:], flat[:, 0:(BT - t) * E],
                                         start=False, stop=False, skip_group_check=True)
                    for t in range(BT):
                        last = nc.tensor.matmul(ps[:, GB, BT * E:(BT + 1) * E], ones[:], oh[:, t, :],
                                                start=False, stop=(t == BT - 1), skip_group_check=True)
                    last.then_inc(count_done, 1)

            def body(b, s, counted=True):
                for c in range(NC):
                    behind(b - 1, 1 - s, c)
                    if counted:
                        count(b - 2, c)
                    chunk(b, s, c)

            pe.wait_ge(w1l_done, 1)
            body(1, 1, counted=False)
            with pe.Fori(1, NB // 2) as i:
                body(i * 2, 0)
                body(i * 2 + 1, 1)
            for c in range(NC):
                behind(NB - 1, 1, c)
                count(NB - 2, c)
            for c in range(NC):
                count(NB - 1, c)

            def turn2(i, s):
                pe.wait_ge(n2_done, i + 1)
                for t in range(2):
                    last = nc.tensor.transpose(ps[:, T2B + s, t * P:(t + 1) * P], tail0[:, s, t * D:(t + 1) * D], ident)
                last.then_inc(t2_done, 1)

            def hidden2(i, s):
                pe.wait_ge(xl2_done, i + 1)
                if not (isinstance(i, int) and i < 2):
                    pe.wait_ge(gelu2_done, i * KH - KH)
                for h in range(KH):
                    hs = slice(h * P, (h + 1) * P)
                    last = split_product(ps[:, H2B + 2 * s + h // 2, (h % 2) * 2 * P:(h % 2 + 1) * 2 * P],
                                         w1h[:, hs], w1l[:, hs], xh2[:, s, :], xl2[:, s, :], start=True, stop=True)
                last.then_inc(h2_done, 1)

            def expert(i, s):
                pe.wait_ge(hl_done, i + 1)
                if not (isinstance(i, int) and i < 2):
                    pe.wait_ge(out_done, i - 1)
                for t in range(2):
                    e = pe.value_load(tab[0:1, 1, bass.ds(i * 2 + t, 1)], min_val=0, max_val=(E - 1) * D)
                    dst = ps[:, YB + s, t * D:(t + 1) * D]
                    for k in range(KH):
                        ts = slice(t * P, (t + 1) * P)
                        split_product(dst, hh[:, s, k, ts], hl[:, s, k, ts], wdh[:, k, bass.ds(e, D)],
                                      wdl[:, k, bass.ds(e, D)], start=(k == 0), stop=False)
                    nc.tensor.matmul(dst, pick0[:], bdh[:, bass.ds(e, D)], start=False, stop=False)
                    last = nc.tensor.matmul(dst, pick0[:], bdl[:, bass.ds(e, D)], start=False, stop=True)
                last.then_inc(y_done, 1)

            pe.wait_ge(gelu_done, NB * KH)
            pe.wait_ge(run_done, NB)
            turn2(0, 0)
            turn2(1, 1)
            hidden2(0, 0)
            pe.wait_ge(xl2_done, 1)
            turn2(2, 0)
            hidden2(1, 1)

            def steps2(i, s, t_ok=True, h_ok=True):
                expert(i, s)
                if h_ok:
                    hidden2(i + 2, s)
                if t_ok:
                    pe.wait_ge(xl2_done, i + 2)
                    turn2(i + 3, 1 - s)

            pe.wait_ge(wdl_done, 1)
            pe.wait_ge(bdl_done, 1)
            pe.wait_ge(tab_done, 1)
            steps2(0, 0)
            steps2(1, 1)
            with pe.Fori(1, PAIRS // 2 - 2) as i:
                steps2(i * 2, 0)
                steps2(i * 2 + 1, 1)
            for i in range(PAIRS - 4, PAIRS):
                steps2(i, i % 2, t_ok=i + 3 < PAIRS, h_ok=i + 2 < PAIRS)


def _constants():
    import numpy as np

    c = np.zeros((P, C_LEN), np.float32)
    c[:, C_ID:C_ID + P] = np.eye(P)
    c[:, C_TRI:C_TRI + P] = np.triu(np.ones((P, P)), 1)
    c[:, C_ONE:C_ONE + P] = 1
    c[:, C_IOTA:C_IOTA + E] = np.arange(E)
    c[:, C_BASE:C_BASE + E + 1] = np.arange(E + 1) * REGION
    c[:, C_HALF:C_HALF + BT] = -0.5
    c[:, C_E:C_E + BT * E] = np.e
    c[:, C_P] = np.arange(P)
    c[:, C_J:C_J + MAXT] = np.arange(MAXT)
    c[0, C_ROW0:C_ROW0 + P] = 1
    tokens = np.arange(N, dtype=np.int32).reshape(N // P, P).T.copy()
    return c, tokens


def kernel(**inputs):
    import numpy as np
    import concourse.bacc as bacc
    from concourse.bass_utils import run_bass_kernel_spmd

    a = {k: np.asarray(v) for k, v in inputs.items()}
    consts, tokens = _constants()
    arrays = {
        "adj": a["adj"].reshape(NB, BN, NC, G, P).transpose(0, 2, 4, 3, 1).reshape(NB * NC * P, G * BN),
        "x": a["x"].reshape(NB, BT, P, D).transpose(0, 2, 1, 3).reshape(NB * P, BT * D),
        "w12": a["L0_gnn_weight"].reshape(2, D, D).transpose(1, 0, 2).reshape(D, 2 * D),
        "gnn_b": a["L0_gnn_bias"],
        "w1": a["L0_ffn_W1"],
        "b1": a["L0_ffn_b1"].reshape(KH, P).T,
        "wg": a["L0_ffn_Wg"].reshape(KH, P, E).transpose(1, 0, 2).reshape(P, KH * E),
        "bg": a["L0_ffn_bg"],
        "wd": a["L0_ffn_Wd"].reshape(E, KH, P, D).transpose(2, 1, 0, 3).reshape(P, KH * E * D),
        "bd": a["L0_ffn_bd"].reshape(E * D),
        "consts": consts,
        "tokens": tokens,
    }
    arrays = {k: np.ascontiguousarray(v) for k, v in arrays.items()}
    nc = bacc.Bacc("TRN2", target_bir_lowering=False, num_devices=1)
    args = [nc.dram_tensor(f"in_{k}", v.shape, mybir.dt.from_np(v.dtype), kind="ExternalInput").ap()
            for k, v in arrays.items()]
    order = ["x", "adj", "w12", "gnn_b", "w1", "b1", "wg", "bg", "wd", "bd", "consts", "tokens"]
    by = dict(zip(arrays, args))
    out = nc.dram_tensor("out", (N, D), F32, kind="ExternalOutput").ap()
    bass_gnn_moe_kernel(nc, *[by[k] for k in order], out)
    r = run_bass_kernel_spmd(nc, [{f"in_{k}": v for k, v in arrays.items()}], core_ids=[0])
    return r.results[0]["out"]
```

```python
from contextlib import ExitStack

import concourse.bass as bass
from concourse import mybir

F32 = mybir.dt.float32
F32R = mybir.dt.float32r
BF16 = mybir.dt.bfloat16
I32 = mybir.dt.int32
U32 = mybir.dt.uint32
ALU = mybir.AluOpType
ACT = mybir.ActivationFunctionType
AX_X = mybir.AxisListType.X

P = 128
N = 8192
D = 128
HID = 512
E = 8
BT = 4
BN = BT * P
NB = N // BN
KH = HID // P
G = 4
NC = N // P // G
RAW = 4
HC = 2
GH = G // HC
NH = NC * HC
HL = 4
XS = 4
REGION = N + P
ROW = D + 4
DUMMY = E * REGION
MAXT = N // P + E
assert MAXT % 24 == 0
PAIRS = MAXT // 2
EPS = 1e-5
PASS = 4
RING = 6

C_ID, C_TRI, C_ONE = 0, P, 2 * P
C_IOTA = 3 * P
C_BASE = C_IOTA + E
C_HALF = C_BASE + E + 1
C_E = C_HALF + BT
C_P = C_E + BT * E
C_J = C_P + 1
C_ROW0 = C_J + MAXT
C_UPTO = C_ROW0 + P
C_LEN = C_UPTO + E * E


def bass_gnn_moe_kernel(nc, x, adj, w12, gnn_b, w1, b1, wg, bg, wd, bd, consts, tokens, out):
    with ExitStack() as ctx:
        def sb(name, shape, dt=F32, stack=ctx):
            return stack.enter_context(nc.sbuf_tensor(name, shape, dt))

        def sem(name):
            return ctx.enter_context(nc.semaphore(name))

        buckets = nc.dram_tensor("buckets", [DUMMY + P, ROW], F32, kind="Internal").ap()

        ps = ctx.enter_context(nc.psum_tensor("ps", [P, 8, 512], F32))
        AGG, TB, HB, GB, ZB = 0, 2, 3, 5, (6, 3)
        H2B, T2B, YB = 0, 4, 6

        cst = sb("cst", [P, C_LEN])
        tri = sb("tri", [P, P], BF16)
        ones = sb("ones", [P, P], BF16)
        w1h = sb("w1h", [P, HID], F32R)
        w1l = sb("w1l", [P, HID], F32R)
        b1c = sb("b1c", [P, KH])
        run = sb("run", [P, E + 1])
        ident = cst[:, C_ID:C_ID + P]

        one = ExitStack()
        raw = sb("raw", [P, RAW, HC, GH * BN], stack=one)
        zh = sb("zh", [P, N], F32R, one)
        zl = sb("zl", [P, N], F32R, one)
        hi = sb("hi", [P, HL, GH * BN], F32R, one)
        lo = sb("lo", [P, HL, GH * BN], F32R, one)
        u = sb("u", [P, N], F32, one)
        xg = sb("xg", [P, XS, BN], F32, one)
        hid = sb("hid", [P, KH, BN], F32, one)
        w1raw = hid[:, 0, :]
        turned = sb("turned", [P, BN], F32, one)
        pre = sb("pre", [P, BN], F32, one)
        xn = sb("xn", [P, 2, BT, D], F32, one)
        xh = sb("xh", [P, BN], F32R, one)
        xl = sb("xl", [P, BN], F32R, one)
        rows = sb("rows", [P, 2, BT, ROW], F32, one)
        padrows = sb("padrows", [P, ROW], F32, one)
        w12s = sb("w12s", [P, 2 * D], F32, one)
        wgs = sb("wgs", [P, KH, E], F32, one)
        gbb = sb("gbb", [P, D], F32, one)
        bgb = sb("bgb", [P, E], F32, one)
        tok = sb("tok", [P, N // P], I32, one)
        st = sb("st", [P, BT, 6], F32, one)
        ms = sb("ms", [P, 2, BT], F32, one)
        md = sb("md", [P, BT], F32, one)
        vs = sb("vs", [P, BT], F32, one)
        ve = sb("ve", [P, BT], F32, one)
        rs = sb("rs", [P, 2, BT], F32, one)
        nm = sb("nm", [P, 2, BT], F32, one)
        lg = sb("lg", [P, BT, E], F32, one)
        mx = sb("mx", [P, BT], F32, one)
        df = sb("df", [P, BT, E], F32, one)
        ex = sb("ex", [P, BT, E], F32, one)
        cand = sb("cand", [P, BT, E], F32, one)
        first = sb("first", [P, BT], F32, one)
        oh = sb("oh", [P, BT, E], BF16, one)
        sm = sb("sm", [P, BT], F32, one)
        place = sb("place", [P, BT, E], F32, one)
        slotf = sb("slotf", [P, BT], F32, one)
        slot = sb("slot", [P, 2, BT], U32, one)
        padslot = sb("padslot", [P, E + 1], I32, one)
        one.close()

        two = ctx
        wdraw = sb("wdraw", [P, KH * E * D], F32, two)
        rows2 = sb("rows2", [P, RING, 2, ROW], F32, two)
        tail0 = sb("tail0", [P, 2, 2 * D], F32, two)
        nt = sb("nt", [P, E], F32, two)
        cnt = sb("cnt", [P, E], I32, two)
        cnt2 = sb("cnt2", [P, E], I32, two)
        upto = sb("upto", [P, E, E], F32, two)
        end = sb("end", [P, E], F32, two)
        past = sb("past", [P, MAXT, E], F32, two)
        pastn = sb("pastn", [P, MAXT, E], F32, two)
        ej = sb("ej", [P, MAXT], F32, two)
        sj = sb("sj", [P, MAXT], F32, two)
        used = sb("used", [P, MAXT], F32, two)
        rj = sb("rj", [P, MAXT], F32, two)
        tab = sb("tab", [P, 2, MAXT], I32, two)
        assert KH * E * D == 2 * G * BN
        fill = sb("fill", [P, (RAW * G * BN - KH * E * D - RING * 2 * ROW - 4 * D - 4 * E - E * E
                               - 2 * MAXT * E - 6 * MAXT)], F32, two)
        wd2 = sb("wd2", [P, KH * E, 2, D], F32R, two)
        bdb = sb("bdb", [P, E * D], F32, two)
        xh2 = sb("xh2", [P, 2, 2 * P], F32R, two)
        xl2 = sb("xl2", [P, 2, 2 * P], F32R, two)
        hid2 = sb("hid2", [P, 2, KH, 2 * P], F32, two)
        hh = sb("hh", [P, 2, KH, 2 * P], F32R, two)
        hl = sb("hl", [P, 2, KH, 2 * P], F32R, two)
        ids = sb("ids", [P, 2, 2], U32, two)
        bd2 = sb("bd2", [P, E, 2, D], F32R, two)
        half2 = sb("half2", [P, 2, 2, D], F32, two)
        pick0 = sb("pick0", [P, P], F32R, two)
        o2 = sb("o2", [P, 2, 2, D], F32, two)

        raw_in = [sem(f"raw_in{s}") for s in range(RAW)]
        xg_in = [sem(f"xg_in{s}") for s in range(XS)]
        cst_in, w12_in, gb_in, w1_in, w_in = sem("cst_in"), sem("w12_in"), sem("gb_in"), sem("w1_in"), sem("w_in")
        cast_done, w1h_done, w1l_done, pad_done = sem("cast_done"), sem("w1h_done"), sem("w1l_done"), sem("pad_done")
        hi_done, lo_done, part_done = sem("hi_done"), sem("lo_done"), sem("part_done")
        bn_done, parts_done, var_done = sem("bn_done"), sem("parts_done"), sem("var_done")
        ve_done, rs_done = sem("ve_done"), sem("rs_done")
        nm_done, xn_done, xnt_done = sem("nm_done"), sem("xn_done"), sem("xnt_done")
        turned_done, zu_done, zh_done, zl_done = sem("turned_done"), sem("zu_done"), sem("zh_done"), sem("zl_done")
        agt_done, ag_turned, pre_done, x2_done = sem("agt_done"), sem("ag_turned"), sem("pre_done"), sem("x2_done")
        xh_done, xl_done, h_done, gelu_done = sem("xh_done"), sem("xl_done"), sem("h_done"), sem("gelu_done")
        gate_done, lg_done, mx_done, df_done = sem("gate_done"), sem("lg_done"), sem("mx_done"), sem("df_done")
        ex_done, less_done, cand_done, first_done = sem("ex_done"), sem("less_done"), sem("cand_done"), sem("first_done")
        oh_done, sum_done, prob_done, count_done = sem("oh_done"), sem("sum_done"), sem("prob_done"), sem("count_done")
        at_done, pick_done, slotf_done, slot_done = sem("at_done"), sem("pick_done"), sem("slotf_done"), sem("slot_done")
        run_done, scattered = sem("run_done"), sem("scattered")
        padslot_done, padded, step_done, tab_done = sem("padslot_done"), sem("padded"), sem("step_done"), sem("tab_done")
        wd_in, bd_in, wdh_done, wdl_done = sem("wd_in"), sem("bd_in"), sem("wdh_done"), sem("wdl_done")
        rows_in = [sem(f"rows_in{s}") for s in range(RING)]
        n2_done, t2_done, xh2_done, xl2_done = sem("n2_done"), sem("t2_done"), sem("xh2_done"), sem("xl2_done")
        h2_done, gelu2_done, hh_done, hl_done = sem("h2_done"), sem("gelu2_done"), sem("hh_done"), sem("hl_done")
        y_done, half_done, out_done = sem("y_done"), sem("half_done"), sem("out_done")
        bdh_done, bdl_done, pick_in = sem("bdh_done"), sem("bdl_done"), sem("pick_in")
        o_done = [sem(f"o_done{s}") for s in range(RING)]
        stored = [sem("stored0"), sem("stored1")]

        def ln_index(q):
            return q + NC

        def pad_regions(eng, experts):
            for e in experts:
                r = eng.value_load(padslot[0:1, e:e + 1], min_val=0, max_val=DUMMY)
                eng.dma_start(buckets[bass.ds(r, P), :], padrows[:]).then_inc(padded, 16)

        block = ctx.enter_context(nc.Block())

        @block.sync
        def _(sp):
            def load_x(slot_, g, nth):
                sp.dma_start(xg[:, slot_, :], x[bass.ds(g * P, P), :]).then_inc(xg_in[slot_], 16)

            def load_chunk(b, c):
                if not (isinstance(b, int) and b == 0 and c < RAW):
                    sp.wait_ge(lo_done, b * NH + (c - RAW + 1) * HC)
                sp.dma_start(raw[:, c % RAW, :, :].rearrange("p h n -> p (h n)"), adj[bass.ds((b * NC + c) * P, P), :]).then_inc(raw_in[c % RAW], 16)

            load_x(0, 0, 0)
            sp.dma_start(cst[:], consts).then_inc(cst_in, 16)
            for g in range(1, XS):
                load_x(g, g, 0)
            for c in range(NC):
                load_chunk(0, c)
                g = c + XS
                if g < NC:
                    sp.wait_ge(xn_done, g - XS + 1)
                    load_x(g % XS, g, g // XS)

            def block_loads(b, s):
                for c in range(NC):
                    load_chunk(b, c)
                    if c == 0:
                        if isinstance(b, int):
                            sp.wait_ge(xn_done, NC)
                            if b >= 3:
                                sp.wait_ge(x2_done, b - 2)
                        else:
                            sp.wait_ge(x2_done, b - 2)
                        load_x(s, b - 1, 0)

            block_loads(1, 0)
            block_loads(2, 1)
            with sp.Fori(1, NB // 2 - 1) as i:
                block_loads(i * 2 + 1, 0)
                block_loads(i * 2 + 2, 1)
            block_loads(NB - 1, 0)
            sp.wait_ge(x2_done, NB - 2)
            load_x(1, NB - 1, 0)
            sp.wait_ge(pad_done, 1)
            sp.dma_start(buckets[DUMMY:DUMMY + P, :], padrows[:]).then_inc(padded, 16)
            sp.wait_ge(lo_done, NB * NH - (RAW - 2) * HC)
            sp.dma_start(wdraw[:], wd).then_inc(wd_in, 16)
            sp.wait_ge(part_done, NB * NH)
            sp.dma_start(bdb[:], bd.partition_broadcast(P)).then_inc(bd_in, 16)

            def load_rows(k, nth, i):
                for t in range(2):
                    r = sp.value_load(tab[0:1, 0, bass.ds(i * 2 + t, 1)], min_val=0, max_val=DUMMY)
                    sp.dma_start(rows2[:, k, t, :], buckets[bass.ds(r, P), :]).then_inc(rows_in[k], 16)

            sp.wait_ge(pad_done, 1)
            sp.wait_ge(padslot_done, 1)
            pad_regions(sp, range(E // 2))

            sp.wait_ge(tab_done, 1)
            sp.wait_ge(scattered, 16 * BT * NB)
            sp.wait_ge(padded, 16 * (E + 1))
            for k in range(RING):
                load_rows(k, 0, k)
            with sp.Fori(1, PAIRS // RING) as i:
                for k in range(RING):
                    sp.wait_ge(o_done[k], i)
                    load_rows(k, 0, i * RING + k)

        @block.scalar
        def _(act):
            def split_hi(b, c):
                act.wait_ge(raw_in[c % RAW], (b * (NC // RAW) + c // RAW + 1) * 16)
                for h in range(HC):
                    j = c * HC + h
                    if not (isinstance(b, int) and b == 0 and j < HL):
                        act.wait_ge(part_done, b * NH + (j - HL + 1))
                    act.copy(hi[:, j % HL, :], raw[:, c % RAW, h, :]).then_inc(hi_done, 1)

            def start_apply(g):
                act.wait_ge(nm_done, g + 1)
                if g >= 2:
                    act.wait_ge(xnt_done, g - 1)
                for t in range(BT):
                    last = act.activation(xn[:, g % 2, t, :], xg[:, g % XS, t * D:(t + 1) * D], ACT.Identity,
                                          bias=nm[:, g % 2, t:t + 1], scale=rs[:, g % 2, t:t + 1])
                last.then_inc(xn_done, 1)

            def turned_copy(g):
                act.wait_ge(xnt_done, g + 1)
                if g >= 1:
                    act.wait_ge(zu_done, g)
                act.copy(turned[:], ps[:, TB, :]).then_inc(turned_done, 1)

            def z_hi(g):
                act.wait_ge(zu_done, g + 1)
                act.copy(zh[:, g * BN:(g + 1) * BN].rearrange("p (t d) -> p t d", t=BT),
                         ps[:, ZB[g % 2]:ZB[g % 2] + 2, :].rearrange("p a (b d) -> p (a b) d", b=4)[:, 1::2, :]
                         ).then_inc(zh_done, 1)

            act.dma_start(w12s[:], w12).then_inc(w12_in, 16)
            act.dma_start(gbb[:], gnn_b.partition_broadcast(P)).then_inc(gb_in, 16)
            act.dma_start(w1raw, w1).then_inc(w1_in, 16)
            act.dma_start(b1c[:], b1).then_inc(w_in, 16)
            act.dma_start(bgb[:], bg.partition_broadcast(P)).then_inc(w_in, 16)
            act.dma_start(wgs[:].rearrange("p k e -> p (k e)"), wg).then_inc(w_in, 16)
            act.dma_start(tok[:], tokens).then_inc(w_in, 16)
            start_apply(0)
            start_apply(1)
            turned_copy(0)
            start_apply(2)
            turned_copy(1)
            z_hi(0)
            start_apply(3)
            split_hi(0, 0)
            for c in range(NC):
                if c + 1 < NC:
                    z_hi(c + 1)
                if c + 2 < NC:
                    turned_copy(c + 2)
                if c + 1 < NC:
                    split_hi(0, c + 1)
                if c + 4 < NC:
                    start_apply(c + 4)
            act.wait_ge(w1_in, 16)
            act.copy(w1h[:], w1raw).then_inc(w1h_done, 1)
            act.wait_ge(w_in, 16 * 4)

            def aggregate_copy(q, s):
                act.wait_ge(part_done, q * NH + NH)
                act.copy(turned[:], ps[:, AGG + s, :]).then_inc(agt_done, 1)

            def ln_hi(q):
                act.wait_ge(xnt_done, ln_index(q) + 1)
                act.copy(xh[:], ps[:, TB, :]).then_inc(xh_done, 1)

            def block_norm(q, s):
                act.wait_ge(nm_done, ln_index(q) + 1)
                for t in range(BT):
                    last = act.activation(xn[:, 0, t, :], rows[:, s, t, 0:D], ACT.Identity,
                                          bias=nm[:, 0, t:t + 1], scale=rs[:, 0, t:t + 1])
                last.then_inc(xn_done, 1)

            def gelu(q, h):
                act.wait_ge(h_done, q * KH + (h + 1))
                act.activation(hid[:, h, :], ps[:, HB + h % 2, :], ACT.Gelu, bias=b1c[:, h:h + 1]).then_inc(gelu_done, 1)

            def behind(q, s, c):
                if c == 1:
                    aggregate_copy(q, s)
                if c == 7:
                    block_norm(q, s)
                if c == 10:
                    ln_hi(q)
                if c == 13:
                    gelu(q, 0)
                    gelu(q, 1)
                if c == 15:
                    gelu(q, 2)
                    gelu(q, 3)

            def body(b, s):
                for c in range(NC):
                    behind(b - 1, 1 - s, c)
                    split_hi(b, c)

            body(1, 1)
            with act.Fori(1, NB // 2) as i:
                body(i * 2, 0)
                body(i * 2 + 1, 1)
            for c in range(NC):
                behind(NB - 1, (NB - 1) % 2, c)
                if c == 1:
                    act.wait_ge(wd_in, 16)
                    act.copy(wd2[:, :, 0, :], wdraw[:].rearrange("p (k d) -> p k d", d=D)).then_inc(wdh_done, 1)
                if c == 7:
                    act.wait_ge(bd_in, 16)
                    act.copy(bd2[:, :, 0, :], bdb[:].rearrange("p (e d) -> p e d", d=D)).then_inc(bdh_done, 1)
                    act.copy(pick0[:], cst[:, C_ROW0:C_ROW0 + P]).then_inc(pick_in, 1)
            act.wait_ge(df_done, NB)
            act.activation(ex[:], df[:], ACT.Exp).then_inc(ex_done, 1)

            act.wait_ge(padslot_done, 1)
            pad_regions(act, range(E // 2, E))

            def ln_hi2(i, s):
                act.wait_ge(t2_done, i + 1)
                act.copy(xh2[:, s, :], ps[:, T2B + s, 0:2 * P]).then_inc(xh2_done, 1)

            def hidden_hi(i, s):
                act.wait_ge(h2_done, i + 1)
                if not (isinstance(i, int) and i < 2):
                    act.wait_ge(hl_done, i * 2 - 2)
                for h in range(KH):
                    act.activation(hid2[:, s, h, :], ps[:, H2B + 2 * s + h // 2, (h % 2) * 2 * P:(h % 2 + 1) * 2 * P],
                                   ACT.Gelu, bias=b1c[:, h:h + 1]).then_inc(gelu2_done, 1)
                    if h == 2:
                        act.wait_ge(gelu2_done, i * KH + 2)
                        if not (isinstance(i, int) and i < 2):
                            act.wait_ge(y_done, i - 1)
                        act.copy(hh[:, s, 0:2, :], hid2[:, s, 0:2, :]).then_inc(hh_done, 1)
                act.wait_ge(gelu2_done, i * KH + KH)
                act.copy(hh[:, s, 2:4, :], hid2[:, s, 2:4, :]).then_inc(hh_done, 1)

            ln_hi2(0, 0)
            ln_hi2(1, 1)
            hidden_hi(0, 0)
            ln_hi2(2, 0)
            hidden_hi(1, 1)
            with act.Fori(1, PAIRS // 2 - 1) as i:
                ln_hi2(i * 2 + 1, 1)
                hidden_hi(i * 2, 0)
                ln_hi2(i * 2 + 2, 0)
                hidden_hi(i * 2 + 1, 1)
            ln_hi2(PAIRS - 1, 1)
            hidden_hi(PAIRS - 2, 0)
            hidden_hi(PAIRS - 1, 1)

        @block.vector
        def _(dve):
            dve.wait_ge(cst_in, 16)
            nc.vector.tensor_copy(tri[:], cst[:, C_TRI:C_TRI + P])
            nc.vector.tensor_copy(ones[:], cst[:, C_ONE:C_ONE + P])
            nc.vector.tensor_copy(run[:], cst[:, C_BASE:C_BASE + E + 1]).then_inc(cast_done, 1)

            def split_lo(b, c):
                for h in range(HC):
                    j = c * HC + h
                    dve.wait_ge(hi_done, b * NH + (j + 1))
                    nc.vector.tensor_tensor(lo[:, j % HL, :], raw[:, c % RAW, h, :], hi[:, j % HL, :].bitcast(F32),
                                            ALU.subtract).then_inc(lo_done, 1)

            def ln_stats(n, tile, v=0):
                for t in range(BT):
                    last = nc.vector.bn_stats(st[:, t, :], tile(t))
                last.then_inc(bn_done, 1)
                dve.wait_ge(bn_done, n + 1)
                nc.vector.tensor_tensor(ms[:, v, :], st[:, :, 1], st[:, :, 4], ALU.add)
                nc.vector.tensor_tensor(md[:], st[:, :, 1], st[:, :, 4], ALU.subtract)
                nc.vector.tensor_tensor(vs[:], st[:, :, 2], st[:, :, 5], ALU.add).then_inc(parts_done, 1)
                dve.wait_ge(parts_done, n + 1)
                nc.vector.scalar_tensor_tensor(out=md[:], in0=md[:], scalar=0.25, in1=md[:],
                                               op0=ALU.mult, op1=ALU.mult)
                nc.vector.tensor_scalar(vs[:], vs[:], 1.0 / D, EPS, ALU.mult, ALU.add).then_inc(var_done, 1)
                dve.wait_ge(var_done, n + 1)
                nc.vector.tensor_tensor(ve[:], md[:], vs[:], ALU.add).then_inc(ve_done, 1)

            def ln_scalars(n, v=0):
                dve.wait_ge(rs_done, n + 1)
                nc.vector.scalar_tensor_tensor(out=nm[:, v, :], in0=ms[:, v, :], scalar=-0.5, in1=rs[:, v, :],
                                               op0=ALU.mult, op1=ALU.mult).then_inc(nm_done, 1)

            def x_tile(g):
                return lambda t: xg[:, g % XS, t * D:(t + 1) * D]

            def start_stats(g):
                dve.wait_ge(xg_in[g % XS], 16 * (g // XS + 1))
                ln_stats(g, x_tile(g), g % 2)

            def z_lo(g):
                dve.wait_ge(zh_done, g + 1)
                if g == 0:
                    dve.wait_ge(gb_in, 16)
                zu = ps[:, ZB[g % 2]:ZB[g % 2] + 2, :].rearrange("p a (b d) -> p (a b) d", b=4)
                nc.vector.tensor_tensor(u[:, g * BN:(g + 1) * BN].rearrange("p (t d) -> p t d", t=BT), zu[:, 0::2, :],
                                        gbb[:].unsqueeze(1).to_broadcast([P, BT, D]), ALU.add)
                sl = slice(g * BN, (g + 1) * BN)
                nc.vector.tensor_tensor(zl[:, sl].rearrange("p (t d) -> p t d", t=BT), zu[:, 1::2, :],
                                        zh[:, sl].bitcast(F32).rearrange("p (t d) -> p t d", t=BT),
                                        ALU.subtract).then_inc(zl_done, 1)

            start_stats(0)
            ln_scalars(0, 0)
            start_stats(1)
            ln_scalars(1, 1)
            start_stats(2)
            ln_scalars(2, 0)
            start_stats(3)
            ln_scalars(3, 1)
            start_stats(4)
            z_lo(0)
            for c in range(NC):
                split_lo(0, c)
                if c + 1 < NC:
                    z_lo(c + 1)
                if c + 4 < NC:
                    ln_scalars(c + 4, c % 2)
                if c + 5 < NC:
                    start_stats(c + 5)
            dve.wait_ge(w1h_done, 1)
            nc.vector.tensor_tensor(w1l[:], w1raw, w1h[:].bitcast(F32), ALU.subtract).then_inc(w1l_done, 1)

            def residual(q, s):
                dve.wait_ge(ag_turned, q + 1)
                nc.vector.tensor_tensor(pre[:], ps[:, TB, :], u[:, bass.ds(q * BN, BN)], ALU.add).then_inc(pre_done, 1)
                if isinstance(q, int):
                    dve.wait_ge(xg_in[s], 16 * (NC // XS + q // 2 + 1))
                dve.wait_ge(pre_done, q + 1)
                if not (isinstance(q, int) and q < 2):
                    dve.wait_ge(scattered, (q - 1) * (16 * BT))
                nc.vector.scalar_tensor_tensor(out=rows[:, s, :, 0:D], in0=pre[:].rearrange("p (t d) -> p t d", t=BT),
                                               scalar=0.0, in1=xg[:, s, :].rearrange("p (t d) -> p t d", t=BT),
                                               op0=ALU.max, op1=ALU.add).then_inc(x2_done, 1)

            def x2_tile(s):
                return lambda t: rows[:, s, t, 0:D]

            def ln_lo(q, s):
                dve.wait_ge(xh_done, q + 1)
                nc.vector.tensor_tensor(xl[:], ps[:, TB, :], xh[:].bitcast(F32), ALU.subtract).then_inc(xl_done, 1)

            def row_scalars(q, s):
                dve.wait_ge(nm_done, ln_index(q) + 1)
                nc.vector.tensor_copy(rows[:, s, :, D], rs[:, 0, :])
                nc.vector.tensor_copy(rows[:, s, :, D + 1], nm[:, 0, :])

            def behind(q, s, c, xcount):
                if c == 4:
                    dve.wait_ge(xg_in[s], xcount)
                    residual(q, s)
                if c == 5:
                    dve.wait_ge(x2_done, q + 1)
                    ln_stats(ln_index(q), x2_tile(s))
                if c == 6:
                    ln_scalars(ln_index(q))
                if c == 7:
                    row_scalars(q, s)
                if c == 11:
                    ln_lo(q, s)

            def route(r, s, c):
                four = ps[:, GB, 0:BT * E].rearrange("p (t e) -> p t e", t=BT)
                iota = cst[:, C_IOTA:C_IOTA + E].unsqueeze(1).to_broadcast([P, BT, E])
                if c == 7:
                    dve.wait_ge(w_in, 16 * 4)
                    dve.wait_ge(gate_done, r + 1)
                    nc.vector.tensor_tensor(lg[:], four, bgb[:].unsqueeze(1).to_broadcast([P, BT, E]),
                                            ALU.add).then_inc(lg_done, 1)
                if c == 8:
                    dve.wait_ge(lg_done, r + 1)
                    nc.vector.tensor_reduce(mx[:], lg[:], AX_X, ALU.max).then_inc(mx_done, 1)
                    dve.wait_ge(mx_done, r + 1)
                    nc.vector.tensor_tensor(df[:], lg[:], mx[:].unsqueeze(2).to_broadcast([P, BT, E]),
                                            ALU.subtract).then_inc(df_done, 1)
                if c == 9:
                    dve.wait_ge(df_done, r + 1)
                    nc.vector.tensor_scalar(cand[:], df[:], 0.0, float(E), ALU.is_lt, ALU.mult).then_inc(less_done, 1)
                    dve.wait_ge(less_done, r + 1)
                    nc.vector.tensor_tensor(cand[:], cand[:], iota, ALU.add).then_inc(cand_done, 1)
                    dve.wait_ge(cand_done, r + 1)
                    nc.vector.tensor_reduce(first[:], cand[:], AX_X, ALU.min).then_inc(first_done, 1)
                if c == 10:
                    dve.wait_ge(first_done, r + 1)
                    nc.vector.tensor_tensor(oh[:], iota, first[:].unsqueeze(2).to_broadcast([P, BT, E]),
                                            ALU.is_equal).then_inc(oh_done, 1)
                if c == 12:
                    dve.wait_ge(ex_done, r + 1)
                    nc.vector.tensor_reduce(sm[:], ex[:], AX_X, ALU.add).then_inc(sum_done, 1)
                    dve.wait_ge(sum_done, r + 1)
                    nc.vector.reciprocal(rows[:, s, :, D + 2], sm[:]).then_inc(prob_done, 1)
                if c == 13:
                    dve.wait_ge(count_done, r + 1)
                    nc.vector.tensor_tensor(place[:], four, run[:, 0:E].unsqueeze(1).to_broadcast([P, BT, E]),
                                            ALU.add).then_inc(at_done, 1)
                    nc.vector.tensor_copy(rows[:, s, :, D + 3].bitcast(I32), tok[:, bass.ds(r * BT, BT)])
                if c == 14:
                    dve.wait_ge(at_done, r + 1)
                    nc.vector.tensor_tensor(place[:], place[:], oh[:], ALU.mult).then_inc(pick_done, 1)
                    nc.vector.tensor_tensor(run[:, 0:E], run[:, 0:E], ps[:, GB, BT * E:(BT + 1) * E],
                                            ALU.add).then_inc(run_done, 1)
                    dve.wait_ge(pick_done, r + 1)
                    nc.vector.tensor_reduce(slotf[:], place[:], AX_X, ALU.add).then_inc(slotf_done, 1)
                    dve.wait_ge(slotf_done, r + 1)
                    nc.vector.tensor_copy(slot[:, s, :], slotf[:]).then_inc(slot_done, 1)

            def body(b, s, xcount, routed=True):
                for c in range(NC):
                    behind(b - 1, 1 - s, c, xcount)
                    if routed:
                        route(b - 2, s, c)
                    split_lo(b, c)

            starts = NC // XS
            body(1, 1, 16 * (starts + 1), routed=False)
            with dve.Fori(1, NB // 2) as i:
                body(i * 2, 0, (i + starts) * 16)
                body(i * 2 + 1, 1, (i + (starts + 1)) * 16)
            for c in range(NC):
                behind(NB - 1, 1, c, 16 * (starts + NB // 2))
                route(NB - 2, 0, c)
            dve.wait_ge(wdh_done, 1)
            nc.vector.tensor_tensor(wd2[:, :, 1, :], wdraw[:].rearrange("p (k d) -> p k d", d=D),
                                    wd2[:, :, 0, :].bitcast(F32), ALU.subtract).then_inc(wdl_done, 1)
            dve.wait_ge(bdh_done, 1)
            nc.vector.tensor_tensor(bd2[:, :, 1, :], bdb[:].rearrange("p (e d) -> p e d", d=D),
                                    bd2[:, :, 0, :].bitcast(F32), ALU.subtract).then_inc(bdl_done, 1)
            for c in range(NC):
                route(NB - 1, 1, c)

            dve.wait_ge(run_done, NB)
            nc.vector.tensor_copy(padslot[:], run[:]).then_inc(padslot_done, 1)

            steps = [0]

            def then(ins):
                ins.then_inc(step_done, 1)
                steps[0] += 1
                dve.wait_ge(step_done, steps[0])

            dve.wait_ge(lo_done, NB * NH)
            then(nc.vector.tensor_tensor(nt[:], run[:, 0:E], cst[:, C_BASE:C_BASE + E], ALU.subtract))
            then(nc.vector.tensor_scalar(cnt[:], nt[:], float(P - 1), None, ALU.add))
            then(nc.vector.tensor_scalar(cnt2[:], cnt[:], 7, None, ALU.arith_shift_right))
            then(nc.vector.tensor_copy(nt[:], cnt2[:]))
            then(nc.vector.tensor_tensor(upto[:], cst[:, C_UPTO:C_UPTO + E * E].rearrange("p (a b) -> p a b", a=E),
                                         nt[:].unsqueeze(1).to_broadcast([P, E, E]), ALU.mult))
            then(nc.vector.tensor_reduce(end[:], upto[:], AX_X, ALU.add))
            js = cst[:, C_J:C_J + MAXT]
            then(nc.vector.tensor_tensor(past[:], js.unsqueeze(2).to_broadcast([P, MAXT, E]),
                                         end[:].unsqueeze(1).to_broadcast([P, MAXT, E]), ALU.is_ge))
            nc.vector.tensor_reduce(ej[:], past[:], AX_X, ALU.add)
            then(nc.vector.tensor_tensor(pastn[:], past[:], nt[:].unsqueeze(1).to_broadcast([P, MAXT, E]), ALU.mult))
            then(nc.vector.tensor_reduce(sj[:], pastn[:], AX_X, ALU.add))
            nc.vector.tensor_scalar(used[:], ej[:], float(E), float(P), ALU.is_lt, ALU.mult)
            then(nc.vector.tensor_tensor(sj[:], js, sj[:], ALU.subtract))
            then(nc.vector.tensor_tensor(sj[:], sj[:], used[:], ALU.mult))
            then(nc.vector.scalar_tensor_tensor(out=rj[:], in0=ej[:], scalar=float(REGION), in1=sj[:],
                                                op0=ALU.mult, op1=ALU.add))
            nc.vector.tensor_copy(tab[:, 0, :], rj[:])
            then(nc.vector.tensor_scalar(ej[:], ej[:], float(E - 1), float(2 * D), ALU.min, ALU.mult))
            nc.vector.tensor_copy(tab[:, 1, :], ej[:]).then_inc(tab_done, 1)

            def normalise2(i, k, rcount):
                dve.wait_ge(rows_in[k], rcount)
                if not (isinstance(i, int) and i < 2):
                    dve.wait_ge(t2_done, i - 1)
                for t in range(2):
                    last = nc.vector.tensor_scalar(tail0[:, k % 2, t * D:(t + 1) * D], rows2[:, k, t, 0:D],
                                                   rows2[:, k, t, D:D + 1], rows2[:, k, t, D + 1:D + 2],
                                                   ALU.mult, ALU.add)
                last.then_inc(n2_done, 1)

            def ln_lo2(i, s):
                dve.wait_ge(xh2_done, i + 1)
                nc.vector.tensor_tensor(xl2[:, s, :], ps[:, T2B + s, 0:2 * P], xh2[:, s, :].bitcast(F32),
                                        ALU.subtract).then_inc(xl2_done, 1)

            def hidden_lo(i, s):
                for j in range(2):
                    js = slice(j * KH // 2, (j + 1) * KH // 2)
                    dve.wait_ge(hh_done, i * 2 + (j + 1))
                    nc.vector.tensor_tensor(hl[:, s, js, :], hid2[:, s, js, :], hh[:, s, js, :].bitcast(F32),
                                            ALU.subtract).then_inc(hl_done, 1)

            def combine(i, k, ocount):
                s = k % 2
                dve.wait_ge(y_done, i + 1)
                if ocount is not None:
                    dve.wait_ge(stored[s], ocount)
                for t in range(2):
                    last = nc.vector.scalar_tensor_tensor(out=half2[:, s, t, :], in0=ps[:, YB + s, t * 2 * D:t * 2 * D + D],
                                                          scalar=rows2[:, k, t, D + 2:D + 3],
                                                          in1=rows2[:, k, t, 0:D], op0=ALU.mult, op1=ALU.add)
                last.then_inc(half_done, 1)
                dve.wait_ge(half_done, i + 1)
                for t in range(2):
                    last = nc.vector.scalar_tensor_tensor(out=o2[:, s, t, :],
                                                          in0=ps[:, YB + s, t * 2 * D + D:(t + 1) * 2 * D],
                                                          scalar=rows2[:, k, t, D + 2:D + 3],
                                                          in1=half2[:, s, t, :], op0=ALU.mult, op1=ALU.add)
                last.then_inc(out_done, 1)
                nc.vector.tensor_copy(ids[:, s, :], rows2[:, k, :, D + 3].bitcast(U32)).then_inc(o_done[k], 1)

            normalise2(0, 0, 32)
            normalise2(1, 1, 32)
            ln_lo2(0, 0)
            normalise2(2, 2, 32)
            ln_lo2(1, 1)
            hidden_lo(0, 0)

            def steps2(i, r, k, c_ok=True, n_ok=True, t_ok=True, h_ok=True, ocount=None):
                if t_ok:
                    ln_lo2(i + 2, k % 2)
                if n_ok:
                    normalise2(i + 3, (k + 3) % RING, (r + (k + 3) // RING + 1) * 32)
                if c_ok:
                    combine(i - 1, (k - 1) % RING, ocount)
                if h_ok:
                    hidden_lo(i + 1, (k + 1) % 2)

            def o_count(r, k):
                return r * (32 * RING // 2) + 32 * ((k - 3) // 2 + 1)

            for k in range(RING):
                steps2(k, 0, k, c_ok=k >= 1, ocount=o_count(0, k) if k >= 3 else None)
            with dve.Fori(1, PAIRS // RING - 1) as i:
                for k in range(RING):
                    steps2(i * RING + k, i, k, ocount=o_count(i, k))
            last_r = PAIRS // RING - 1
            for k in range(RING):
                i = last_r * RING + k
                steps2(i, last_r, k, n_ok=i + 3 < PAIRS, t_ok=i + 2 < PAIRS, h_ok=i + 1 < PAIRS,
                       ocount=o_count(last_r, k))
            combine(PAIRS - 1, RING - 1, o_count(last_r, RING))

        @block.gpsimd
        def _(pool):
            def rstd(n, v=0):
                pool.wait_ge(ve_done, n + 1)
                nc.gpsimd.tensor_tensor(rs[:, v, :], ve[:], cst[:, C_HALF:C_HALF + BT], ALU.pow).then_inc(rs_done, 1)

            def exps(r):
                pool.wait_ge(df_done, r + 1)
                nc.gpsimd.tensor_tensor(ex[:].rearrange("p t e -> p (t e)"), cst[:, C_E:C_E + BT * E],
                                        df[:].rearrange("p t e -> p (t e)"), ALU.pow).then_inc(ex_done, 1)

            def scatter(r, s):
                pool.wait_ge(cst_in, 16)
                pool.wait_ge(slot_done, r + 1)
                pool.wait_ge(prob_done, r + 1)
                for t in range(BT):
                    nc.gpsimd.indirect_dma_start(
                        out=buckets, out_offset=bass.IndirectOffsetOnAxis(ap=slot[:, s, t:t + 1], axis=0),
                        in_=rows[:, s, t, :], in_offset=None).then_inc(scattered, 16)

            nc.gpsimd.memset(padrows[:, 0:D + 3], 0.0)
            nc.gpsimd.memset(padrows[:, D + 3:ROW].bitcast(I32), N).then_inc(pad_done, 1)
            pool.wait_ge(cst_in, 16)
            for g in range(NC):
                if g >= 2:
                    pool.wait_ge(xn_done, g - 1)
                rstd(g, g % 2)
            rstd(ln_index(0))
            with pool.Fori(1, NB // 2) as i:
                for s in range(2):
                    r = i * 2 + (s - 2)
                    rstd(ln_index(r + 1))
                    exps(r)
                    scatter(r, s)
            rstd(ln_index(NB - 1))
            exps(NB - 2)
            scatter(NB - 2, 0)
            scatter(NB - 1, 1)

            def store(r, k):
                pool.wait_ge(cst_in, 16)
                pool.wait_ge(o_done[k], r)
                for t in range(2):
                    nc.gpsimd.indirect_dma_start(
                        out=out, out_offset=bass.IndirectOffsetOnAxis(
                            ap=ids[:, k % 2, t:t + 1], axis=0),
                        in_=o2[:, k % 2, t, :], in_offset=None,
                        bounds_check=N - 1, oob_is_err=False).then_inc(stored[k % 2], 16)

            with pool.Fori(1, PAIRS // RING + 1) as i:
                for k in range(RING):
                    store(i, k)
            pool.wait_ge(stored[0], 16 * PAIRS)
            pool.wait_ge(stored[1], 16 * PAIRS)

        @block.tensor
        def _(pe):
            def split_product(dst, ah, al, bh, bl, start, stop):
                nc.tensor.matmul(dst, ah, bh, start=start, stop=False)
                nc.tensor.matmul(dst, ah, bl, start=False, stop=False)
                return nc.tensor.matmul(dst, al, bh, start=False, stop=stop)

            def chunk(b, s, c):
                for j in range(c * HC, (c + 1) * HC):
                    pe.wait_ge(lo_done, b * NH + (j + 1))
                    for g in range(GH):
                        k = j * GH + g
                        zs, ns = slice(k * P, (k + 1) * P), slice(g * BN, (g + 1) * BN)
                        last = split_product(ps[:, AGG + s, :], zh[:, zs], zl[:, zs], hi[:, j % HL, ns],
                                             lo[:, j % HL, ns], start=(k == 0), stop=(k == G * NC - 1))
                    last.then_inc(part_done, 1)

            def turn_norm(n, v=0):
                pe.wait_ge(xn_done, n + 1)
                for t in range(BT):
                    last = nc.tensor.transpose(ps[:, TB, t * P:(t + 1) * P], xn[:, v, t, :], ident)
                last.then_inc(xnt_done, 1)

            def z_and_u(g):
                pe.wait_ge(turned_done, g + 1)
                if g >= 2:
                    pe.wait_ge(zl_done, g - 1)
                for t in range(BT):
                    last = nc.tensor.matmul(ps[:, ZB[g % 2] + t // 2, (t % 2) * 2 * D:(t % 2 + 1) * 2 * D],
                                            turned[:, t * P:(t + 1) * P], w12s[:], start=True, stop=True)
                last.then_inc(zu_done, 1)

            pe.wait_ge(cst_in, 16)
            turn_norm(0, 0)
            pe.wait_ge(w12_in, 16)
            pe.wait_ge(turned_done, 1)
            turn_norm(1, 1)
            z_and_u(0)
            pe.wait_ge(turned_done, 2)
            turn_norm(2, 0)
            z_and_u(1)
            for c in range(NC):
                pe.wait_ge(zl_done, c + 1)
                chunk(0, 0, c)
                if c + 3 < NC:
                    pe.wait_ge(turned_done, c + 3)
                    turn_norm(c + 3, (c + 3) % 2)
                if c + 2 < NC:
                    z_and_u(c + 2)

            def behind(q, s, c):
                if c == 2:
                    pe.wait_ge(agt_done, q + 1)
                    for t in range(BT):
                        last = nc.tensor.transpose(ps[:, TB, t * P:(t + 1) * P], turned[:, t * P:(t + 1) * P], ident)
                    last.then_inc(ag_turned, 1)
                if c == 8:
                    turn_norm(ln_index(q))
                if c in (11, 13):
                    for h in range(c - 11, c - 9):
                        pe.wait_ge(xl_done, q + 1)
                        if c == 13:
                            pe.wait_ge(gelu_done, q * KH + (h - 1))
                        hs = slice(h * P, (h + 1) * P)
                        split_product(ps[:, HB + h % 2, :], w1h[:, hs], w1l[:, hs], xh[:], xl[:],
                                      start=True, stop=True).then_inc(h_done, 1)

            def gate_and_count(r, c):
                if 2 <= c < 2 + KH:
                    h = c - 2
                    pe.wait_ge(w_in, 16 * 4)
                    pe.wait_ge(gelu_done, r * KH + (h + 1))
                    for t in range(BT):
                        last = nc.tensor.matmul(ps[:, GB, t * E:(t + 1) * E], hid[:, h, t * P:(t + 1) * P],
                                                wgs[:, h, :], start=(h == 0 and t == 0), stop=(h == KH - 1),
                                                skip_group_check=True)
                    if h == KH - 1:
                        last.then_inc(gate_done, 1)
                if c == 11:
                    pe.wait_ge(oh_done, r + 1)
                    flat = oh[:].rearrange("p t e -> p (t e)")
                    nc.tensor.matmul(ps[:, GB, 0:BT * E], tri[:], flat, start=True, stop=False, skip_group_check=True)
                    for t in range(1, BT):
                        nc.tensor.matmul(ps[:, GB, t * E:BT * E], ones[:], flat[:, 0:(BT - t) * E],
                                         start=False, stop=False, skip_group_check=True)
                    for t in range(BT):
                        last = nc.tensor.matmul(ps[:, GB, BT * E:(BT + 1) * E], ones[:], oh[:, t, :],
                                                start=False, stop=(t == BT - 1), skip_group_check=True)
                    last.then_inc(count_done, 1)

            def body(b, s, counted=True):
                for c in range(NC):
                    behind(b - 1, 1 - s, c)
                    if counted:
                        gate_and_count(b - 2, c)
                    chunk(b, s, c)

            pe.wait_ge(w1l_done, 1)
            body(1, 1, counted=False)
            with pe.Fori(1, NB // 2) as i:
                body(i * 2, 0)
                body(i * 2 + 1, 1)
            for c in range(NC):
                behind(NB - 1, 1, c)
                gate_and_count(NB - 2, c)
            pe.wait_ge(run_done, NB - 1)
            for c in range(NC):
                gate_and_count(NB - 1, c)

            def turn2(i, s):
                pe.wait_ge(n2_done, i + 1)
                for t in range(2):
                    last = nc.tensor.transpose(ps[:, T2B + s, t * P:(t + 1) * P], tail0[:, s, t * D:(t + 1) * D], ident)
                last.then_inc(t2_done, 1)

            def hidden2(i, s):
                pe.wait_ge(xl2_done, i + 1)
                if not (isinstance(i, int) and i < 2):
                    pe.wait_ge(gelu2_done, i * KH - KH)
                for h in range(KH):
                    hs = slice(h * P, (h + 1) * P)
                    last = split_product(ps[:, H2B + 2 * s + h // 2, (h % 2) * 2 * P:(h % 2 + 1) * 2 * P],
                                         w1h[:, hs], w1l[:, hs], xh2[:, s, :], xl2[:, s, :], start=True, stop=True)
                last.then_inc(h2_done, 1)

            def expert(i, s, es):
                pe.wait_ge(hl_done, i * 2 + 1)
                if not (isinstance(i, int) and i < 2):
                    pe.wait_ge(out_done, i - 1)
                for t in range(2):
                    e = es[t]
                    both = ps[:, YB + s, t * 2 * D:(t + 1) * 2 * D]
                    upper = ps[:, YB + s, t * 2 * D:t * 2 * D + D]
                    ts = slice(t * P, (t + 1) * P)
                    for k in range(KH):
                        if t == 0 and k == KH // 2:
                            pe.wait_ge(hl_done, i * 2 + 2)
                        wk = wd2[:, k * E:(k + 1) * E, :, :].rearrange("p e h d -> p (e h d)")
                        nc.tensor.matmul(both, hh[:, s, k, ts], wk[:, bass.ds(e, 2 * D)], start=(k == 0), stop=False)
                        nc.tensor.matmul(upper, hl[:, s, k, ts], wk[:, bass.ds(e, D)], start=False, stop=False)
                    last = nc.tensor.matmul(both, pick0[:], bd2[:].rearrange("p e h d -> p (e h d)")[:, bass.ds(e, 2 * D)],
                                            start=False, stop=True)
                last.then_inc(y_done, 1)

            pe.wait_ge(gelu_done, NB * KH)
            pe.wait_ge(run_done, NB)
            turn2(0, 0)
            turn2(1, 1)
            hidden2(0, 0)
            pe.wait_ge(xl2_done, 1)
            turn2(2, 0)
            hidden2(1, 1)

            def experts_of(i, n):
                _, es = nc.values_load_multi_w_load_instructions(
                    tab[0:1, 1, bass.ds(i * 2, 2 * n)], engines=[mybir.EngineType.PE], min_val=0, max_val=(E - 1) * 2 * D,
                    skip_runtime_bounds_check_because="the table holds min(e, E - 1) * 2 * D, e a sum of comparisons")
                return es

            def steps2(i, s, es, t_ok=True, h_ok=True):
                expert(i, s, es)
                if h_ok:
                    hidden2(i + 2, s)
                if t_ok:
                    pe.wait_ge(xl2_done, i + 2)
                    turn2(i + 3, 1 - s)

            def pass2(i, last=False):
                es = experts_of(i, PASS)
                for k in range(PASS):
                    steps2(i + k, k % 2, es[2 * k:2 * k + 2], t_ok=not last or k + 3 < PASS,
                           h_ok=not last or k + 2 < PASS)

            pe.wait_ge(wdl_done, 1)
            pe.wait_ge(bdl_done, 1)
            pe.wait_ge(pick_in, 1)
            pe.wait_ge(tab_done, 1)
            pass2(0)
            with pe.Fori(1, PAIRS // PASS - 1) as i:
                pass2(i * PASS)
            pass2(PAIRS - PASS, last=True)


def _constants():
    import numpy as np

    c = np.zeros((P, C_LEN), np.float32)
    c[:, C_ID:C_ID + P] = np.eye(P)
    c[:, C_TRI:C_TRI + P] = np.triu(np.ones((P, P)), 1)
    c[:, C_ONE:C_ONE + P] = 1
    c[:, C_IOTA:C_IOTA + E] = np.arange(E)
    c[:, C_BASE:C_BASE + E + 1] = np.arange(E + 1) * REGION
    c[:, C_HALF:C_HALF + BT] = -0.5
    c[:, C_E:C_E + BT * E] = np.e
    c[:, C_P] = np.arange(P)
    c[:, C_J:C_J + MAXT] = np.arange(MAXT)
    c[0, C_ROW0:C_ROW0 + P] = 1
    c[:, C_UPTO:C_UPTO + E * E] = np.tril(np.ones((E, E))).reshape(-1)
    tokens = np.arange(N, dtype=np.int32).reshape(N // P, P).T.copy()
    return c, tokens


def kernel(**inputs):
    import numpy as np
    import concourse.bacc as bacc
    from concourse.bass_utils import run_bass_kernel_spmd

    a = {k: np.asarray(v) for k, v in inputs.items()}
    consts, tokens = _constants()
    arrays = {
        "adj": a["adj"].reshape(NB, BN, NC, G, P).transpose(0, 2, 4, 3, 1).reshape(NB * NC * P, G * BN),
        "x": a["x"].reshape(NB, BT, P, D).transpose(0, 2, 1, 3).reshape(NB * P, BT * D),
        "w12": a["L0_gnn_weight"].reshape(2, D, D).transpose(1, 0, 2).reshape(D, 2 * D),
        "gnn_b": a["L0_gnn_bias"],
        "w1": a["L0_ffn_W1"],
        "b1": a["L0_ffn_b1"].reshape(KH, P).T,
        "wg": a["L0_ffn_Wg"].reshape(KH, P, E).transpose(1, 0, 2).reshape(P, KH * E),
        "bg": a["L0_ffn_bg"],
        "wd": a["L0_ffn_Wd"].reshape(E, KH, P, D).transpose(2, 1, 0, 3).reshape(P, KH * E * D),
        "bd": a["L0_ffn_bd"].reshape(E * D),
        "consts": consts,
        "tokens": tokens,
    }
    arrays = {k: np.ascontiguousarray(v) for k, v in arrays.items()}
    nc = bacc.Bacc("TRN2", target_bir_lowering=False, num_devices=1)
    args = [nc.dram_tensor(f"in_{k}", v.shape, mybir.dt.from_np(v.dtype), kind="ExternalInput").ap()
            for k, v in arrays.items()]
    order = ["x", "adj", "w12", "gnn_b", "w1", "b1", "wg", "bg", "wd", "bd", "consts", "tokens"]
    by = dict(zip(arrays, args))
    out = nc.dram_tensor("out", (N, D), F32, kind="ExternalOutput").ap()
    bass_gnn_moe_kernel(nc, *[by[k] for k in order], out)
    r = run_bass_kernel_spmd(nc, [{f"in_{k}": v for k, v in arrays.items()}], core_ids=[0])
    return r.results[0]["out"]
```

```python
from contextlib import ExitStack

import concourse.bass as bass
from concourse import mybir

F32 = mybir.dt.float32
F32R = mybir.dt.float32r
BF16 = mybir.dt.bfloat16
I32 = mybir.dt.int32
U32 = mybir.dt.uint32
ALU = mybir.AluOpType
ACT = mybir.ActivationFunctionType
AX_X = mybir.AxisListType.X

P = 128
N = 8192
D = 128
HID = 512
E = 8
BT = 4
BN = BT * P
NB = N // BN
KH = HID // P
G = 4
NC = N // P // G
RAW = 4
HC = 2
GH = G // HC
NH = NC * HC
HL = 4
XS = 4
REGION = N + P
ROW = D + 4
DUMMY = E * REGION
MAXT = N // P + E
assert MAXT % 24 == 0
PAIRS = MAXT // 2
EPS = 1e-5
PASS = 4
RING = 6
EARLY = (N - 2 * BN - E * (P - 1)) // P // 24 * 24

C_ID, C_TRI, C_ONE = 0, P, 2 * P
C_IOTA = 3 * P
C_BASE = C_IOTA + E
C_HALF = C_BASE + E + 1
C_E = C_HALF + BT
C_P = C_E + BT * E
C_J = C_P + 1
C_ROW0 = C_J + MAXT
C_UPTO = C_ROW0 + P
C_MEAN = C_UPTO + E * E
C_QUARTER = C_MEAN + BT
C_EPS = C_QUARTER + BT
C_LEN = C_EPS + BT


def bass_gnn_moe_kernel(nc, x, adj, w12, gnn_b, w1, b1, wg, bg, wd, bd, consts, tokens, out):
    with ExitStack() as ctx:
        def sb(name, shape, dt=F32, stack=ctx):
            return stack.enter_context(nc.sbuf_tensor(name, shape, dt))

        def sem(name):
            return ctx.enter_context(nc.semaphore(name))

        buckets = nc.dram_tensor("buckets", [DUMMY + P, ROW], F32, kind="Internal").ap()

        ps = ctx.enter_context(nc.psum_tensor("ps", [P, 8, 512], F32))
        AGG, TB, HB, GB, ZB = 0, 2, 3, 5, (6, 3)
        H2B, YB, T2B = 0, 4, 6

        cst = sb("cst", [P, C_LEN])
        tri = sb("tri", [P, P], BF16)
        ones = sb("ones", [P, P], BF16)
        w1h = sb("w1h", [P, HID], F32R)
        w1l = sb("w1l", [P, HID], F32R)
        b1c = sb("b1c", [P, KH])
        run = sb("run", [P, E + 1])
        ident = cst[:, C_ID:C_ID + P]
        nt = sb("nt", [P, E])
        cnt = sb("cnt", [P, E], I32)
        cnt2 = sb("cnt2", [P, E], I32)
        upto = sb("upto", [P, E, E])
        end = sb("end", [P, E])
        start = sb("start", [P, E])
        taken = sb("taken", [P, E])
        jumps = sb("jumps", [P, E])
        tab = sb("tab", [P, 2, MAXT], I32)

        one = ExitStack()
        raw = sb("raw", [P, RAW, HC, GH * BN], stack=one)
        zh = sb("zh", [P, N], F32R, one)
        zl = sb("zl", [P, N], F32R, one)
        hi = sb("hi", [P, HL, GH * BN], F32R, one)
        lo = sb("lo", [P, HL, GH * BN], F32R, one)
        u = sb("u", [P, N], F32, one)
        xg = sb("xg", [P, XS, BN], F32, one)
        hid = sb("hid", [P, KH, BN], F32, one)
        w1raw = hid[:, 0, :]
        turned = sb("turned", [P, BN], F32, one)
        pre = sb("pre", [P, BN], F32, one)
        scratch = xg[:, 2:4, :].rearrange("p s n -> p (s n)")
        past, pastn = [scratch[:, k * EARLY * E:(k + 1) * EARLY * E].rearrange("p (j e) -> p j e", e=E) for k in range(2)]
        ej, sj, used, rj = [scratch[:, 2 * EARLY * E + k * EARLY:2 * EARLY * E + (k + 1) * EARLY] for k in range(4)]
        assert EARLY >= MAXT - EARLY and EARLY * (2 * E + 4) <= 2 * BN
        xn = sb("xn", [P, 2, BT, D], F32, one)
        xh = sb("xh", [P, BN], F32R, one)
        xl = sb("xl", [P, BN], F32R, one)
        rows = sb("rows", [P, 2, BT, ROW], F32, one)
        padrows = sb("padrows", [P, ROW], F32, one)
        w12s = sb("w12s", [P, 2 * D], F32, one)
        wgs = sb("wgs", [P, KH, E], F32, one)
        gbb = sb("gbb", [P, D], F32, one)
        bgb = sb("bgb", [P, E], F32, one)
        tok = sb("tok", [P, N // P], I32, one)
        st = sb("st", [P, 2, BT, 6], F32, one)
        ms = sb("ms", [P, 2, BT], F32, one)
        md = sb("md", [P, BT], F32, one)
        md2 = sb("md2", [P, BT], F32, one)
        vs = sb("vs", [P, BT], F32, one)
        ve = sb("ve", [P, BT], F32, one)
        rs = sb("rs", [P, 2, BT], F32, one)
        nm = sb("nm", [P, 2, BT], F32, one)
        lg = sb("lg", [P, BT, E], F32, one)
        mx = sb("mx", [P, BT], F32, one)
        df = sb("df", [P, BT, E], F32, one)
        ex = sb("ex", [P, BT, E], F32, one)
        cand = sb("cand", [P, BT, E], F32, one)
        first = sb("first", [P, BT], F32, one)
        oh = sb("oh", [P, BT, E], BF16, one)
        sm = sb("sm", [P, BT], F32, one)
        place = sb("place", [P, BT, E], F32, one)
        slotf = sb("slotf", [P, BT], F32, one)
        slot = sb("slot", [P, 2, BT], U32, one)
        padslot = sb("padslot", [P, E + 1], I32, one)
        one.close()

        two = ctx
        wdraw = sb("wdraw", [P, KH * E * D], F32, two)
        rows2 = sb("rows2", [P, RING, 2, ROW], F32, two)
        tail0 = sb("tail0", [P, 2, 2 * D], F32, two)
        assert KH * E * D == 2 * G * BN
        fill = sb("fill", [P, RAW * G * BN - KH * E * D - RING * 2 * ROW - 4 * D], F32, two)
        wd2 = sb("wd2", [P, KH * E, 2, D], F32R, two)
        bdb = sb("bdb", [P, E * D], F32, two)
        xh2 = sb("xh2", [P, 2, 2 * P], F32R, two)
        xl2 = sb("xl2", [P, 2, 2 * P], F32R, two)
        hid2 = sb("hid2", [P, 2, KH, 2 * P], F32, two)
        hh = sb("hh", [P, 2, KH, 2 * P], F32R, two)
        hl = sb("hl", [P, 2, KH, 2 * P], F32R, two)
        ids = sb("ids", [P, 2, 2], U32, two)
        bd2 = sb("bd2", [P, E, 2, D], F32R, two)
        half2 = sb("half2", [P, 2, 2, D], F32, two)
        pick0 = sb("pick0", [P, P], F32R, two)
        o2 = sb("o2", [P, 2, 2, D], F32, two)

        raw_in = [sem(f"raw_in{s}") for s in range(RAW)]
        xg_in = [sem(f"xg_in{s}") for s in range(XS)]
        cst_in, w12_in, gb_in, w1_in, w_in = sem("cst_in"), sem("w12_in"), sem("gb_in"), sem("w1_in"), sem("w_in")
        w1h_done, w1l_done, pad_done = sem("w1h_done"), sem("w1l_done"), sem("pad_done")
        hi_done, lo_done, part_done = sem("hi_done"), sem("lo_done"), sem("part_done")
        bn_done, parts_done, var_done = sem("bn_done"), sem("parts_done"), sem("var_done")
        md_done, ve_done, rs_done = sem("md_done"), sem("ve_done"), sem("rs_done")
        nm_done, xn_done, xnt_done = sem("nm_done"), sem("xn_done"), sem("xnt_done")
        turned_done, zu_done, zh_done, zl_done = sem("turned_done"), sem("zu_done"), sem("zh_done"), sem("zl_done")
        agt_done, ag_turned, pre_done, x2_done = sem("agt_done"), sem("ag_turned"), sem("pre_done"), sem("x2_done")
        xh_done, xl_done, h_done, gelu_done = sem("xh_done"), sem("xl_done"), sem("h_done"), sem("gelu_done")
        gate_done, lg_done, mx_done, df_done = sem("gate_done"), sem("lg_done"), sem("mx_done"), sem("df_done")
        ex_done, less_done, cand_done, first_done = sem("ex_done"), sem("less_done"), sem("cand_done"), sem("first_done")
        oh_done, sum_done, prob_done, count_done = sem("oh_done"), sem("sum_done"), sem("prob_done"), sem("count_done")
        at_done, pick_done, slotf_done, slot_done = sem("at_done"), sem("pick_done"), sem("slotf_done"), sem("slot_done")
        run_done, scattered = sem("run_done"), sem("scattered")
        padslot_done, padded, step_done, tab_done = sem("padslot_done"), sem("padded"), sem("step_done"), sem("tab_done")
        early_done = sem("early_done")
        wd_in, bd_in, wdh_done, wdl_done = sem("wd_in"), sem("bd_in"), sem("wdh_done"), sem("wdl_done")
        rows_in = [sem(f"rows_in{s}") for s in range(RING)]
        n2_done, t2_done, xh2_done, xl2_done = sem("n2_done"), sem("t2_done"), sem("xh2_done"), sem("xl2_done")
        h2_done, gelu2_done, hh_done, hl_done = sem("h2_done"), sem("gelu2_done"), sem("hh_done"), sem("hl_done")
        y_done, half_done, out_done = sem("y_done"), sem("half_done"), sem("out_done")
        bdh_done, bdl_done, pick_in = sem("bdh_done"), sem("bdl_done"), sem("pick_in")
        o_done = [sem(f"o_done{s}") for s in range(RING)]
        stored = [sem("stored0"), sem("stored1")]

        def ln_index(q):
            return q + NC

        def load_rows(eng, k, i, ts=range(2)):
            for t in ts:
                r = eng.value_load(tab[0:1, 0, bass.ds(i * 2 + t, 1)], min_val=0, max_val=DUMMY)
                eng.dma_start(rows2[:, k, t, :], buckets[bass.ds(r, P), :]).then_inc(rows_in[k], 16)

        def pad_regions(eng, experts):
            for e in experts:
                r = eng.value_load(padslot[0:1, e:e + 1], min_val=0, max_val=DUMMY)
                eng.dma_start(buckets[bass.ds(r, P), :], padrows[:]).then_inc(padded, 16)

        block = ctx.enter_context(nc.Block())

        @block.sync
        def _(sp):
            def load_x(slot_, g):
                sp.dma_start(xg[:, slot_, :], x[bass.ds(g * P, P), :]).then_inc(xg_in[slot_], 16)

            def load_chunk(b, c):
                if not (isinstance(b, int) and b == 0 and c < RAW):
                    sp.wait_ge(lo_done, b * NH + (c - RAW + 1) * HC)
                sp.dma_start(raw[:, c % RAW, :, :].rearrange("p h n -> p (h n)"), adj[bass.ds((b * NC + c) * P, P), :]).then_inc(raw_in[c % RAW], 16)

            load_x(0, 0)
            sp.dma_start(cst[:], consts).then_inc(cst_in, 16)
            sp.dma_start(w12s[:], w12).then_inc(w12_in, 16)
            for g in range(1, XS):
                load_x(g, g)
            for c in range(NC):
                load_chunk(0, c)
                if c == RAW - 1:
                    sp.dma_start(w1raw, w1).then_inc(w1_in, 16)
                    sp.dma_start(b1c[:], b1).then_inc(w_in, 16)
                    sp.dma_start(bgb[:], bg.partition_broadcast(P)).then_inc(w_in, 16)
                    sp.dma_start(wgs[:].rearrange("p k e -> p (k e)"), wg).then_inc(w_in, 16)
                    sp.dma_start(tok[:], tokens).then_inc(w_in, 16)
                g = c + XS
                if g < NC:
                    sp.wait_ge(xn_done, g - XS + 1)
                    load_x(g % XS, g)

            def block_loads(b, s):
                for c in range(NC):
                    load_chunk(b, c)
                    if c == 0:
                        if isinstance(b, int):
                            sp.wait_ge(xn_done, NC)
                            if b >= 3:
                                sp.wait_ge(x2_done, b - 2)
                        else:
                            sp.wait_ge(x2_done, b - 2)
                        load_x(s, b - 1)

            block_loads(1, 0)
            block_loads(2, 1)
            with sp.Fori(1, NB // 2 - 1) as i:
                block_loads(i * 2 + 1, 0)
                block_loads(i * 2 + 2, 1)
            block_loads(NB - 1, 0)
            sp.wait_ge(x2_done, NB - 2)
            load_x(1, NB - 1)
            sp.wait_ge(pad_done, 1)
            sp.dma_start(buckets[DUMMY:DUMMY + P, :], padrows[:]).then_inc(padded, 16)
            sp.wait_ge(lo_done, NB * NH - (RAW - 2) * HC)
            sp.dma_start(wdraw[:], wd).then_inc(wd_in, 16)
            sp.wait_ge(part_done, NB * NH)
            sp.dma_start(bdb[:], bd.partition_broadcast(P)).then_inc(bd_in, 16)


            sp.wait_ge(early_done, 1)
            sp.wait_ge(scattered, 16 * BT * (NB - 2))
            for k in range(RING):
                load_rows(sp, k, k)
            def later_rows(i, pads=False):
                for k in range(RING):
                    sp.wait_ge(o_done[k], i)
                    load_rows(sp, k, i * RING + k)
                    if pads:
                        pad_regions(sp, range(k * E // RING, (k + 1) * E // RING))

            sp.wait_ge(padslot_done, 1)
            later_rows(1, pads=True)
            with sp.Fori(2, EARLY // 2 // RING) as i:
                later_rows(i)
            sp.wait_ge(tab_done, 1)
            sp.wait_ge(scattered, 16 * BT * NB)
            sp.wait_ge(padded, 16 * (E + 1))
            with sp.Fori(EARLY // 2 // RING, PAIRS // RING) as i:
                later_rows(i)

        @block.scalar
        def _(act):
            def split_hi(b, c):
                act.wait_ge(raw_in[c % RAW], (b * (NC // RAW) + c // RAW + 1) * 16)
                for h in range(HC):
                    j = c * HC + h
                    if not (isinstance(b, int) and b == 0 and j < HL):
                        act.wait_ge(part_done, b * NH + (j - HL + 1))
                    act.copy(hi[:, j % HL, :], raw[:, c % RAW, h, :]).then_inc(hi_done, 1)

            def start_apply(g):
                act.wait_ge(nm_done, g + 1)
                if g >= 2:
                    act.wait_ge(xnt_done, g - 1)
                for t in range(BT):
                    last = act.activation(xn[:, g % 2, t, :], xg[:, g % XS, t * D:(t + 1) * D], ACT.Identity,
                                          bias=nm[:, g % 2, t:t + 1], scale=rs[:, g % 2, t:t + 1])
                last.then_inc(xn_done, 1)

            def turned_copy(g):
                act.wait_ge(xnt_done, g + 1)
                if g >= 1:
                    act.wait_ge(zu_done, g)
                act.copy(turned[:], ps[:, TB, :]).then_inc(turned_done, 1)

            def z_hi(g):
                act.wait_ge(zu_done, g + 1)
                act.copy(zh[:, g * BN:(g + 1) * BN].rearrange("p (t d) -> p t d", t=BT),
                         ps[:, ZB[g % 2]:ZB[g % 2] + 2, :].rearrange("p a (b d) -> p (a b) d", b=4)[:, 1::2, :]
                         ).then_inc(zh_done, 1)

            start_apply(0)
            act.dma_start(gbb[:], gnn_b.partition_broadcast(P)).then_inc(gb_in, 16)
            turned_copy(0)
            start_apply(1)
            start_apply(2)
            z_hi(0)
            turned_copy(1)
            split_hi(0, 0)
            start_apply(3)
            for c in range(NC):
                if c + 1 < NC:
                    z_hi(c + 1)
                if c + 2 < NC:
                    turned_copy(c + 2)
                if c + 1 < NC:
                    split_hi(0, c + 1)
                if c + 4 < NC:
                    start_apply(c + 4)
            act.wait_ge(w1_in, 16)
            act.copy(w1h[:], w1raw).then_inc(w1h_done, 1)
            act.wait_ge(w_in, 16 * 4)

            def aggregate_copy(q, s):
                act.wait_ge(part_done, q * NH + NH)
                act.copy(turned[:], ps[:, AGG + s, :]).then_inc(agt_done, 1)

            def ln_hi(q):
                act.wait_ge(xnt_done, ln_index(q) + 1)
                act.copy(xh[:], ps[:, TB, :]).then_inc(xh_done, 1)

            def block_norm(q, s):
                act.wait_ge(nm_done, ln_index(q) + 1)
                for t in range(BT):
                    last = act.activation(xn[:, 0, t, :], rows[:, s, t, 0:D], ACT.Identity,
                                          bias=nm[:, 0, t:t + 1], scale=rs[:, 0, t:t + 1])
                last.then_inc(xn_done, 1)

            def gelu(q, h):
                act.wait_ge(h_done, q * KH + (h + 1))
                act.activation(hid[:, h, :], ps[:, HB + h % 2, :], ACT.Gelu, bias=b1c[:, h:h + 1]).then_inc(gelu_done, 1)

            def behind(q, s, c):
                if c == 1:
                    aggregate_copy(q, s)
                if c == 7:
                    block_norm(q, s)
                if c == 10:
                    ln_hi(q)
                if c == 13:
                    gelu(q, 0)
                    gelu(q, 1)
                if c == 15:
                    gelu(q, 2)
                    gelu(q, 3)

            def body(b, s):
                for c in range(NC):
                    behind(b - 1, 1 - s, c)
                    split_hi(b, c)

            body(1, 1)
            with act.Fori(1, NB // 2) as i:
                body(i * 2, 0)
                body(i * 2 + 1, 1)
            def ln_hi2(i, s):
                act.wait_ge(t2_done, i + 1)
                act.copy(xh2[:, s, :], ps[:, T2B + s, 0:2 * P]).then_inc(xh2_done, 1)

            def hidden_hi(i, s):
                act.wait_ge(h2_done, i + 1)
                if not (isinstance(i, int) and i < 2):
                    act.wait_ge(hl_done, i * 2 - 2)
                for h in range(KH):
                    act.activation(hid2[:, s, h, :], ps[:, H2B + 2 * s + h // 2, (h % 2) * 2 * P:(h % 2 + 1) * 2 * P],
                                   ACT.Gelu, bias=b1c[:, h:h + 1]).then_inc(gelu2_done, 1)
                    if h == 2:
                        act.wait_ge(gelu2_done, i * KH + 2)
                        if not (isinstance(i, int) and i < 2):
                            act.wait_ge(y_done, i - 1)
                        act.copy(hh[:, s, 0:2, :], hid2[:, s, 0:2, :]).then_inc(hh_done, 1)
                act.wait_ge(gelu2_done, i * KH + KH)
                act.copy(hh[:, s, 2:4, :], hid2[:, s, 2:4, :]).then_inc(hh_done, 1)

            for c in range(NC):
                behind(NB - 1, (NB - 1) % 2, c)
                if c == 1:
                    act.wait_ge(wd_in, 16)
                    for k in range(KH):
                        ks = slice(k * E, (k + 1) * E)
                        act.copy(wd2[:, ks, 0, :], wdraw[:].rearrange("p (k d) -> p k d", d=D)[:, ks, :]).then_inc(wdh_done, 1)
                if c == 7:
                    act.wait_ge(bd_in, 16)
                    act.copy(bd2[:, :, 0, :], bdb[:].rearrange("p (e d) -> p e d", d=D)).then_inc(bdh_done, 1)
                    act.copy(pick0[:], cst[:, C_ROW0:C_ROW0 + P]).then_inc(pick_in, 1)
                if c == 13:
                    ln_hi2(0, 0)

            ln_hi2(1, 1)
            hidden_hi(0, 0)
            ln_hi2(2, 0)
            hidden_hi(1, 1)
            with act.Fori(1, PAIRS // 2 - 1) as i:
                ln_hi2(i * 2 + 1, 1)
                hidden_hi(i * 2, 0)
                ln_hi2(i * 2 + 2, 0)
                hidden_hi(i * 2 + 1, 1)
            ln_hi2(PAIRS - 1, 1)
            hidden_hi(PAIRS - 2, 0)
            hidden_hi(PAIRS - 1, 1)

        @block.vector
        def _(dve):
            def split_lo(b, c):
                for h in range(HC):
                    j = c * HC + h
                    dve.wait_ge(hi_done, b * NH + (j + 1))
                    nc.vector.tensor_tensor(lo[:, j % HL, :], raw[:, c % RAW, h, :], hi[:, j % HL, :].bitcast(F32),
                                            ALU.subtract).then_inc(lo_done, 1)

            def ln_stats(n, tile, v=0):
                for t in range(BT):
                    last = nc.vector.bn_stats(st[:, v, t, :], tile(t))
                last.then_inc(bn_done, 1)

            def ln_scalars(n, v=0):
                dve.wait_ge(rs_done, n + 1)
                nc.vector.scalar_tensor_tensor(out=nm[:, v, :], in0=ms[:, v, :], scalar=-0.5, in1=rs[:, v, :],
                                               op0=ALU.mult, op1=ALU.mult).then_inc(nm_done, 1)

            def x_tile(g):
                return lambda t: xg[:, g % XS, t * D:(t + 1) * D]

            def start_stats(g):
                dve.wait_ge(xg_in[g % XS], 16 * (g // XS + 1))
                ln_stats(g, x_tile(g), g % 2)

            def z_lo(g):
                dve.wait_ge(zh_done, g + 1)
                if g == 0:
                    dve.wait_ge(gb_in, 16)
                zu = ps[:, ZB[g % 2]:ZB[g % 2] + 2, :].rearrange("p a (b d) -> p (a b) d", b=4)
                nc.vector.tensor_tensor(u[:, g * BN:(g + 1) * BN].rearrange("p (t d) -> p t d", t=BT), zu[:, 0::2, :],
                                        gbb[:].unsqueeze(1).to_broadcast([P, BT, D]), ALU.add)
                sl = slice(g * BN, (g + 1) * BN)
                nc.vector.tensor_tensor(zl[:, sl].rearrange("p (t d) -> p t d", t=BT), zu[:, 1::2, :],
                                        zh[:, sl].bitcast(F32).rearrange("p (t d) -> p t d", t=BT),
                                        ALU.subtract).then_inc(zl_done, 1)

            start_stats(0)
            dve.wait_ge(cst_in, 16)
            nc.vector.tensor_copy(tri[:], cst[:, C_TRI:C_TRI + P])
            nc.vector.tensor_copy(ones[:], cst[:, C_ONE:C_ONE + P])
            nc.vector.tensor_copy(run[:], cst[:, C_BASE:C_BASE + E + 1])
            start_stats(1)
            ln_scalars(0, 0)
            start_stats(2)
            ln_scalars(1, 1)
            start_stats(3)
            ln_scalars(2, 0)
            z_lo(0)
            for c in range(NC):
                if c == 0:
                    ln_scalars(3, 1)
                split_lo(0, c)
                if c == 0:
                    start_stats(4)
                if c + 1 < NC:
                    z_lo(c + 1)
                if c + 4 < NC:
                    ln_scalars(c + 4, c % 2)
                if c + 5 < NC:
                    start_stats(c + 5)
            dve.wait_ge(w1h_done, 1)
            nc.vector.tensor_tensor(w1l[:], w1raw, w1h[:].bitcast(F32), ALU.subtract).then_inc(w1l_done, 1)

            def residual(q, s):
                dve.wait_ge(ag_turned, q + 1)
                nc.vector.tensor_tensor(pre[:], ps[:, TB, :], u[:, bass.ds(q * BN, BN)], ALU.add).then_inc(pre_done, 1)
                if isinstance(q, int):
                    dve.wait_ge(xg_in[s], 16 * (NC // XS + q // 2 + 1))
                dve.wait_ge(pre_done, q + 1)
                if not (isinstance(q, int) and q < 2):
                    dve.wait_ge(scattered, (q - 1) * (16 * BT))
                nc.vector.scalar_tensor_tensor(out=rows[:, s, :, 0:D], in0=pre[:].rearrange("p (t d) -> p t d", t=BT),
                                               scalar=0.0, in1=xg[:, s, :].rearrange("p (t d) -> p t d", t=BT),
                                               op0=ALU.max, op1=ALU.add).then_inc(x2_done, 1)

            def x2_tile(s):
                return lambda t: rows[:, s, t, 0:D]

            def ln_lo(q, s):
                dve.wait_ge(xh_done, q + 1)
                nc.vector.tensor_tensor(xl[:], ps[:, TB, :], xh[:].bitcast(F32), ALU.subtract).then_inc(xl_done, 1)

            def row_scalars(q, s):
                dve.wait_ge(nm_done, ln_index(q) + 1)
                nc.vector.tensor_copy(rows[:, s, :, D], rs[:, 0, :])
                nc.vector.tensor_copy(rows[:, s, :, D + 1], nm[:, 0, :])

            def behind(q, s, c, xcount):
                if c == 4:
                    dve.wait_ge(xg_in[s], xcount)
                    residual(q, s)
                if c == 5:
                    dve.wait_ge(x2_done, q + 1)
                    ln_stats(ln_index(q), x2_tile(s))
                if c == 6:
                    ln_scalars(ln_index(q))
                if c == 7:
                    row_scalars(q, s)
                if c == 11:
                    ln_lo(q, s)

            def route(r, s, c):
                four = ps[:, GB, 0:BT * E].rearrange("p (t e) -> p t e", t=BT)
                iota = cst[:, C_IOTA:C_IOTA + E].unsqueeze(1).to_broadcast([P, BT, E])
                if c == 7:
                    dve.wait_ge(w_in, 16 * 4)
                    dve.wait_ge(gate_done, r + 1)
                    nc.vector.tensor_tensor(lg[:], four, bgb[:].unsqueeze(1).to_broadcast([P, BT, E]),
                                            ALU.add).then_inc(lg_done, 1)
                if c == 8:
                    dve.wait_ge(lg_done, r + 1)
                    nc.vector.tensor_reduce(mx[:], lg[:], AX_X, ALU.max).then_inc(mx_done, 1)
                    dve.wait_ge(mx_done, r + 1)
                    nc.vector.tensor_tensor(df[:], lg[:], mx[:].unsqueeze(2).to_broadcast([P, BT, E]),
                                            ALU.subtract).then_inc(df_done, 1)
                if c == 9:
                    dve.wait_ge(df_done, r + 1)
                    nc.vector.tensor_scalar(cand[:], df[:], 0.0, float(E), ALU.is_lt, ALU.mult).then_inc(less_done, 1)
                    dve.wait_ge(less_done, r + 1)
                    nc.vector.tensor_tensor(cand[:], cand[:], iota, ALU.add).then_inc(cand_done, 1)
                    dve.wait_ge(cand_done, r + 1)
                    nc.vector.tensor_reduce(first[:], cand[:], AX_X, ALU.min).then_inc(first_done, 1)
                if c == 10:
                    dve.wait_ge(first_done, r + 1)
                    nc.vector.tensor_tensor(oh[:], iota, first[:].unsqueeze(2).to_broadcast([P, BT, E]),
                                            ALU.is_equal).then_inc(oh_done, 1)
                if c == 12:
                    dve.wait_ge(ex_done, r + 1)
                    nc.vector.tensor_reduce(sm[:], ex[:], AX_X, ALU.add).then_inc(sum_done, 1)
                    dve.wait_ge(sum_done, r + 1)
                    nc.vector.reciprocal(rows[:, s, :, D + 2], sm[:]).then_inc(prob_done, 1)
                if c == 13:
                    dve.wait_ge(count_done, r + 1)
                    nc.vector.tensor_tensor(place[:], four, run[:, 0:E].unsqueeze(1).to_broadcast([P, BT, E]),
                                            ALU.add).then_inc(at_done, 1)
                    nc.vector.tensor_copy(rows[:, s, :, D + 3].bitcast(I32), tok[:, bass.ds(r * BT, BT)])
                if c == 14:
                    dve.wait_ge(at_done, r + 1)
                    nc.vector.tensor_tensor(place[:], place[:], oh[:], ALU.mult).then_inc(pick_done, 1)
                    nc.vector.tensor_tensor(run[:, 0:E], run[:, 0:E], ps[:, GB, BT * E:(BT + 1) * E],
                                            ALU.add).then_inc(run_done, 1)
                    dve.wait_ge(pick_done, r + 1)
                    nc.vector.tensor_reduce(slotf[:], place[:], AX_X, ALU.add).then_inc(slotf_done, 1)
                    dve.wait_ge(slotf_done, r + 1)
                    nc.vector.tensor_copy(slot[:, s, :], slotf[:]).then_inc(slot_done, 1)

            def body(b, s, xcount, routed=True):
                for c in range(NC):
                    behind(b - 1, 1 - s, c, xcount)
                    if routed:
                        route(b - 2, s, c)
                    split_lo(b, c)

            starts = NC // XS
            body(1, 1, 16 * (starts + 1), routed=False)
            with dve.Fori(1, NB // 2) as i:
                body(i * 2, 0, (i + starts) * 16)
                body(i * 2 + 1, 1, (i + (starts + 1)) * 16)
            steps = [0]

            def then(ins):
                ins.then_inc(step_done, 1)
                steps[0] += 1
                dve.wait_ge(step_done, steps[0])

            def tiles_of_experts(slack):
                then(nc.vector.tensor_tensor(nt[:], run[:, 0:E], cst[:, C_BASE:C_BASE + E], ALU.subtract))
                then(nc.vector.tensor_scalar(cnt[:], nt[:], float(slack), None, ALU.add))
                then(nc.vector.tensor_scalar(cnt2[:], cnt[:], 7, None, ALU.arith_shift_right))
                then(nc.vector.tensor_copy(nt[:], cnt2[:]))

            def ends():
                then(nc.vector.tensor_tensor(upto[:], cst[:, C_UPTO:C_UPTO + E * E].rearrange("p (a b) -> p a b", a=E),
                                             nt[:].unsqueeze(1).to_broadcast([P, E, E]), ALU.mult))
                then(nc.vector.tensor_reduce(end[:], upto[:], AX_X, ALU.add))

            def experts_of_tiles(n, hops):
                then(nc.vector.tensor_tensor(past[:, 0:n], cst[:, C_J:C_J + n].unsqueeze(2).to_broadcast([P, n, E]),
                                             end[:].unsqueeze(1).to_broadcast([P, n, E]), ALU.is_ge))
                nc.vector.tensor_reduce(ej[:, 0:n], past[:, 0:n], AX_X, ALU.add)
                then(nc.vector.tensor_tensor(pastn[:, 0:n], past[:, 0:n], hops[:].unsqueeze(1).to_broadcast([P, n, E]),
                                             ALU.mult))

            def offsets_of_tiles(n, lead):
                then(nc.vector.tensor_reduce(sj[:, 0:n], pastn[:, 0:n], AX_X, ALU.add))
                nc.vector.tensor_scalar(used[:, 0:n], ej[:, 0:n], float(E), float(P), ALU.is_lt, ALU.mult)
                then(nc.vector.tensor_tensor(sj[:, 0:n], cst[:, C_J:C_J + n], sj[:, 0:n], ALU.subtract))
                then(nc.vector.scalar_tensor_tensor(out=sj[:, 0:n], in0=sj[:, 0:n], scalar=lead, in1=used[:, 0:n],
                                                    op0=ALU.add, op1=ALU.mult))

            def rows_of_tiles(first, n, done):
                then(nc.vector.scalar_tensor_tensor(out=rj[:, 0:n], in0=ej[:, 0:n], scalar=float(REGION),
                                                    in1=sj[:, 0:n], op0=ALU.mult, op1=ALU.add))
                nc.vector.tensor_copy(tab[:, 0, first:first + n], rj[:, 0:n])
                then(nc.vector.tensor_scalar(ej[:, 0:n], ej[:, 0:n], float(E - 1), float(2 * D), ALU.min, ALU.mult))
                nc.vector.tensor_copy(tab[:, 1, first:first + n], ej[:, 0:n]).then_inc(done, 1)

            def early_table(part):
                if part == 0:
                    tiles_of_experts(0)
                    ends()
                if part == 1:
                    experts_of_tiles(EARLY, nt)
                if part == 2:
                    offsets_of_tiles(EARLY, 0.0)
                    rows_of_tiles(0, EARLY, early_done)
                if part == 3:
                    then(nc.vector.tensor_tensor(start[:], end[:], nt[:], ALU.subtract))
                    then(nc.vector.tensor_scalar(start[:], start[:], float(EARLY), None, ALU.min))
                    then(nc.vector.scalar_tensor_tensor(out=taken[:], in0=end[:], scalar=float(EARLY), in1=start[:],
                                                        op0=ALU.min, op1=ALU.subtract))

            def late_table(part):
                if part == 0:
                    tiles_of_experts(P - 1)
                if part == 1:
                    then(nc.vector.tensor_copy(jumps[:], nt[:]))
                    then(nc.vector.tensor_tensor(nt[:], nt[:], taken[:], ALU.subtract))
                    ends()
                if part == 2:
                    then(nc.vector.tensor_tensor(jumps[:, 0:E - 1], jumps[:, 0:E - 1], taken[:, 1:E], ALU.subtract))
                    experts_of_tiles(MAXT - EARLY, jumps)
                if part == 3:
                    offsets_of_tiles(MAXT - EARLY, taken[:, 0:1])
                if part == 4:
                    rows_of_tiles(EARLY, MAXT - EARLY, tab_done)

            def normalise2(i, k, rcount):
                dve.wait_ge(rows_in[k], rcount)
                if not (isinstance(i, int) and i < 2):
                    dve.wait_ge(t2_done, i - 1)
                for t in range(2):
                    last = nc.vector.tensor_scalar(tail0[:, k % 2, t * D:(t + 1) * D], rows2[:, k, t, 0:D],
                                                   rows2[:, k, t, D:D + 1], rows2[:, k, t, D + 1:D + 2],
                                                   ALU.mult, ALU.add)
                last.then_inc(n2_done, 1)

            def ln_lo2(i, s):
                dve.wait_ge(xh2_done, i + 1)
                nc.vector.tensor_tensor(xl2[:, s, :], ps[:, T2B + s, 0:2 * P], xh2[:, s, :].bitcast(F32),
                                        ALU.subtract).then_inc(xl2_done, 1)

            def hidden_lo(i, s):
                for j in range(2):
                    js = slice(j * KH // 2, (j + 1) * KH // 2)
                    dve.wait_ge(hh_done, i * 2 + (j + 1))
                    nc.vector.tensor_tensor(hl[:, s, js, :], hid2[:, s, js, :], hh[:, s, js, :].bitcast(F32),
                                            ALU.subtract).then_inc(hl_done, 1)

            def combine(i, k, ocount):
                s = k % 2
                dve.wait_ge(y_done, i + 1)
                if ocount is not None:
                    dve.wait_ge(stored[s], ocount)
                for t in range(2):
                    last = nc.vector.scalar_tensor_tensor(out=half2[:, s, t, :], in0=ps[:, YB + s, t * 2 * D:t * 2 * D + D],
                                                          scalar=rows2[:, k, t, D + 2:D + 3],
                                                          in1=rows2[:, k, t, 0:D], op0=ALU.mult, op1=ALU.add)
                last.then_inc(half_done, 1)
                dve.wait_ge(half_done, i + 1)
                for t in range(2):
                    last = nc.vector.scalar_tensor_tensor(out=o2[:, s, t, :],
                                                          in0=ps[:, YB + s, t * 2 * D + D:(t + 1) * 2 * D],
                                                          scalar=rows2[:, k, t, D + 2:D + 3],
                                                          in1=half2[:, s, t, :], op0=ALU.mult, op1=ALU.add)
                last.then_inc(out_done, 1)
                nc.vector.tensor_copy(ids[:, s, :], rows2[:, k, :, D + 3].bitcast(U32)).then_inc(o_done[k], 1)

            def wd_lo(k):
                ks = slice(k * E, (k + 1) * E)
                dve.wait_ge(wdh_done, k + 1)
                nc.vector.tensor_tensor(wd2[:, ks, 1, :], wdraw[:].rearrange("p (k d) -> p k d", d=D)[:, ks, :],
                                        wd2[:, ks, 0, :].bitcast(F32), ALU.subtract).then_inc(wdl_done, 1)

            early_table(0)
            early_table(1)
            for c in range(NC):
                behind(NB - 1, 1, c, 16 * (starts + NB // 2))
                route(NB - 2, 0, c)
                if c == 5:
                    early_table(2)
                if c == 10:
                    wd_lo(0)
                if c == 11:
                    wd_lo(1)
                    normalise2(0, 0, 32)
                    wd_lo(2)
                if c == 14:
                    normalise2(1, 1, 32)
                    ln_lo2(0, 0)
            wd_lo(3)
            dve.wait_ge(bdh_done, 1)
            nc.vector.tensor_tensor(bd2[:, :, 1, :], bdb[:].rearrange("p (e d) -> p e d", d=D),
                                    bd2[:, :, 0, :].bitcast(F32), ALU.subtract).then_inc(bdl_done, 1)
            ln_lo2(1, 1)
            normalise2(2, 2, 32)
            hidden_lo(0, 0)
            for c in range(11):
                route(NB - 1, 1, c)

            def steps2(i, r, k, c_ok=True, n_ok=True, t_ok=True, h_ok=True, ocount=None):
                if t_ok:
                    ln_lo2(i + 2, k % 2)
                if n_ok:
                    normalise2(i + 3, (k + 3) % RING, (r + (k + 3) // RING + 1) * 32)
                if c_ok:
                    combine(i - 1, (k - 1) % RING, ocount)
                if h_ok:
                    hidden_lo(i + 1, (k + 1) % 2)

            def o_count(r, k):
                return r * (32 * RING // 2) + 32 * ((k - 3) // 2 + 1)

            for k in range(RING):
                steps2(k, 0, k, c_ok=k >= 1, ocount=o_count(0, k) if k >= 3 else None)
                if k == 0:
                    route(NB - 1, 1, 13)
                    route(NB - 1, 1, 14)
                    dve.wait_ge(run_done, NB)
                    nc.vector.tensor_copy(padslot[:], run[:]).then_inc(padslot_done, 1)
                    route(NB - 1, 1, 12)
                if k == 1:
                    early_table(3)
                if k >= 1:
                    late_table(k - 1)
            with dve.Fori(1, PAIRS // RING - 1) as i:
                for k in range(RING):
                    steps2(i * RING + k, i, k, ocount=o_count(i, k))
            last_r = PAIRS // RING - 1
            for k in range(RING):
                i = last_r * RING + k
                steps2(i, last_r, k, n_ok=i + 3 < PAIRS, t_ok=i + 2 < PAIRS, h_ok=i + 1 < PAIRS,
                       ocount=o_count(last_r, k))
            combine(PAIRS - 1, RING - 1, o_count(last_r, RING))

        @block.gpsimd
        def _(pool):
            def rstd(n, v=0):
                pool.wait_ge(bn_done, n + 1)
                nc.gpsimd.tensor_tensor(ms[:, v, :], st[:, v, :, 1], st[:, v, :, 4], ALU.add)
                nc.gpsimd.tensor_tensor(md[:], st[:, v, :, 1], st[:, v, :, 4], ALU.subtract)
                nc.gpsimd.tensor_tensor(vs[:], st[:, v, :, 2], st[:, v, :, 5], ALU.add).then_inc(parts_done, 1)
                pool.wait_ge(parts_done, n + 1)
                nc.gpsimd.tensor_tensor(md2[:], md[:], md[:], ALU.mult)
                nc.gpsimd.tensor_tensor(ve[:], vs[:], cst[:, C_MEAN:C_MEAN + BT], ALU.mult).then_inc(var_done, 1)
                pool.wait_ge(var_done, n + 1)
                nc.gpsimd.tensor_tensor(md[:], md2[:], cst[:, C_QUARTER:C_QUARTER + BT], ALU.mult)
                nc.gpsimd.tensor_tensor(vs[:], ve[:], cst[:, C_EPS:C_EPS + BT], ALU.add).then_inc(md_done, 1)
                pool.wait_ge(md_done, n + 1)
                nc.gpsimd.tensor_tensor(ve[:], md[:], vs[:], ALU.add).then_inc(ve_done, 1)
                pool.wait_ge(ve_done, n + 1)
                nc.gpsimd.tensor_tensor(rs[:, v, :], ve[:], cst[:, C_HALF:C_HALF + BT], ALU.pow).then_inc(rs_done, 1)

            def exps(r):
                pool.wait_ge(df_done, r + 1)
                nc.gpsimd.tensor_tensor(ex[:].rearrange("p t e -> p (t e)"), cst[:, C_E:C_E + BT * E],
                                        df[:].rearrange("p t e -> p (t e)"), ALU.pow).then_inc(ex_done, 1)

            def scatter(r, s):
                pool.wait_ge(cst_in, 16)
                pool.wait_ge(slot_done, r + 1)
                pool.wait_ge(prob_done, r + 1)
                for t in range(BT):
                    nc.gpsimd.indirect_dma_start(
                        out=buckets, out_offset=bass.IndirectOffsetOnAxis(ap=slot[:, s, t:t + 1], axis=0),
                        in_=rows[:, s, t, :], in_offset=None).then_inc(scattered, 16)

            nc.gpsimd.memset(padrows[:, 0:D + 3], 0.0)
            nc.gpsimd.memset(padrows[:, D + 3:ROW].bitcast(I32), N).then_inc(pad_done, 1)
            pool.wait_ge(cst_in, 16)
            for g in range(NC):
                if g >= 2:
                    pool.wait_ge(xn_done, g - 1)
                rstd(g, g % 2)
            rstd(ln_index(0))
            with pool.Fori(1, NB // 2) as i:
                for s in range(2):
                    r = i * 2 + (s - 2)
                    rstd(ln_index(r + 1))
                    exps(r)
                    scatter(r, s)
            rstd(ln_index(NB - 1))
            exps(NB - 2)
            scatter(NB - 2, 0)
            exps(NB - 1)
            scatter(NB - 1, 1)

            def store(r, k):
                pool.wait_ge(cst_in, 16)
                pool.wait_ge(o_done[k], r)
                for t in range(2):
                    nc.gpsimd.indirect_dma_start(
                        out=out, out_offset=bass.IndirectOffsetOnAxis(
                            ap=ids[:, k % 2, t:t + 1], axis=0),
                        in_=o2[:, k % 2, t, :], in_offset=None,
                        bounds_check=N - 1, oob_is_err=False).then_inc(stored[k % 2], 16)

            with pool.Fori(1, PAIRS // RING + 1) as i:
                for k in range(RING):
                    store(i, k)
            pool.wait_ge(stored[0], 16 * PAIRS)
            pool.wait_ge(stored[1], 16 * PAIRS)

        @block.tensor
        def _(pe):
            def split_product(dst, ah, al, bh, bl, start, stop):
                nc.tensor.matmul(dst, ah, bh, start=start, stop=False)
                nc.tensor.matmul(dst, ah, bl, start=False, stop=False)
                return nc.tensor.matmul(dst, al, bh, start=False, stop=stop)

            def chunk(b, s, c):
                for j in range(c * HC, (c + 1) * HC):
                    pe.wait_ge(lo_done, b * NH + (j + 1))
                    for g in range(GH):
                        k = j * GH + g
                        zs, ns = slice(k * P, (k + 1) * P), slice(g * BN, (g + 1) * BN)
                        last = split_product(ps[:, AGG + s, :], zh[:, zs], zl[:, zs], hi[:, j % HL, ns],
                                             lo[:, j % HL, ns], start=(k == 0), stop=(k == G * NC - 1))
                    last.then_inc(part_done, 1)

            def turn_norm(n, v=0):
                pe.wait_ge(xn_done, n + 1)
                for t in range(BT):
                    last = nc.tensor.transpose(ps[:, TB, t * P:(t + 1) * P], xn[:, v, t, :], ident)
                last.then_inc(xnt_done, 1)

            def z_and_u(g):
                pe.wait_ge(turned_done, g + 1)
                if g >= 2:
                    pe.wait_ge(zl_done, g - 1)
                for t in range(BT):
                    last = nc.tensor.matmul(ps[:, ZB[g % 2] + t // 2, (t % 2) * 2 * D:(t % 2 + 1) * 2 * D],
                                            turned[:, t * P:(t + 1) * P], w12s[:], start=True, stop=True)
                last.then_inc(zu_done, 1)

            pe.wait_ge(cst_in, 16)
            turn_norm(0, 0)
            pe.wait_ge(w12_in, 16)
            z_and_u(0)
            turn_norm(1, 1)
            pe.wait_ge(turned_done, 2)
            turn_norm(2, 0)
            z_and_u(1)
            for c in range(NC):
                pe.wait_ge(zl_done, c + 1)
                chunk(0, 0, c)
                if c + 3 < NC:
                    pe.wait_ge(turned_done, c + 3)
                    turn_norm(c + 3, (c + 3) % 2)
                if c + 2 < NC:
                    z_and_u(c + 2)

            def behind(q, s, c):
                if c == 2:
                    pe.wait_ge(agt_done, q + 1)
                    for t in range(BT):
                        last = nc.tensor.transpose(ps[:, TB, t * P:(t + 1) * P], turned[:, t * P:(t + 1) * P], ident)
                    last.then_inc(ag_turned, 1)
                if c == 8:
                    turn_norm(ln_index(q))
                if c in (11, 13):
                    for h in range(c - 11, c - 9):
                        pe.wait_ge(xl_done, q + 1)
                        if c == 13:
                            pe.wait_ge(gelu_done, q * KH + (h - 1))
                        hs = slice(h * P, (h + 1) * P)
                        split_product(ps[:, HB + h % 2, :], w1h[:, hs], w1l[:, hs], xh[:], xl[:],
                                      start=True, stop=True).then_inc(h_done, 1)

            def gate_and_count(r, c):
                if 2 <= c < 2 + KH:
                    h = c - 2
                    pe.wait_ge(w_in, 16 * 4)
                    pe.wait_ge(gelu_done, r * KH + (h + 1))
                    for t in range(BT):
                        last = nc.tensor.matmul(ps[:, GB, t * E:(t + 1) * E], hid[:, h, t * P:(t + 1) * P],
                                                wgs[:, h, :], start=(h == 0 and t == 0), stop=(h == KH - 1),
                                                skip_group_check=True)
                    if h == KH - 1:
                        last.then_inc(gate_done, 1)
                if c == 11:
                    pe.wait_ge(oh_done, r + 1)
                    flat = oh[:].rearrange("p t e -> p (t e)")
                    nc.tensor.matmul(ps[:, GB, 0:BT * E], tri[:], flat, start=True, stop=False, skip_group_check=True)
                    for t in range(1, BT):
                        nc.tensor.matmul(ps[:, GB, t * E:BT * E], ones[:], flat[:, 0:(BT - t) * E],
                                         start=False, stop=False, skip_group_check=True)
                    for t in range(BT):
                        last = nc.tensor.matmul(ps[:, GB, BT * E:(BT + 1) * E], ones[:], oh[:, t, :],
                                                start=False, stop=(t == BT - 1), skip_group_check=True)
                    last.then_inc(count_done, 1)

            def body(b, s, counted=True):
                for c in range(NC):
                    behind(b - 1, 1 - s, c)
                    if counted:
                        gate_and_count(b - 2, c)
                    chunk(b, s, c)

            pe.wait_ge(w1l_done, 1)
            body(1, 1, counted=False)
            with pe.Fori(1, NB // 2) as i:
                body(i * 2, 0)
                body(i * 2 + 1, 1)
            def turn2(i, s):
                pe.wait_ge(n2_done, i + 1)
                for t in range(2):
                    last = nc.tensor.transpose(ps[:, T2B + s, t * P:(t + 1) * P], tail0[:, s, t * D:(t + 1) * D], ident)
                last.then_inc(t2_done, 1)

            def hidden2(i, s):
                pe.wait_ge(xl2_done, i + 1)
                if not (isinstance(i, int) and i < 2):
                    pe.wait_ge(gelu2_done, i * KH - KH)
                for h in range(KH):
                    hs = slice(h * P, (h + 1) * P)
                    last = split_product(ps[:, H2B + 2 * s + h // 2, (h % 2) * 2 * P:(h % 2 + 1) * 2 * P],
                                         w1h[:, hs], w1l[:, hs], xh2[:, s, :], xl2[:, s, :], start=True, stop=True)
                last.then_inc(h2_done, 1)

            def expert(i, s, es):
                pe.wait_ge(hl_done, i * 2 + 1)
                if not (isinstance(i, int) and i < 2):
                    pe.wait_ge(out_done, i - 1)
                for t in range(2):
                    e = es[t]
                    both = ps[:, YB + s, t * 2 * D:(t + 1) * 2 * D]
                    upper = ps[:, YB + s, t * 2 * D:t * 2 * D + D]
                    ts = slice(t * P, (t + 1) * P)
                    for k in range(KH):
                        if t == 0 and k == KH // 2:
                            pe.wait_ge(hl_done, i * 2 + 2)
                        wk = wd2[:, k * E:(k + 1) * E, :, :].rearrange("p e h d -> p (e h d)")
                        nc.tensor.matmul(both, hh[:, s, k, ts], wk[:, bass.ds(e, 2 * D)], start=(k == 0), stop=False)
                        nc.tensor.matmul(upper, hl[:, s, k, ts], wk[:, bass.ds(e, D)], start=False, stop=False)
                    last = nc.tensor.matmul(both, pick0[:], bd2[:].rearrange("p e h d -> p (e h d)")[:, bass.ds(e, 2 * D)],
                                            start=False, stop=True)
                last.then_inc(y_done, 1)

            for c in range(NC):
                behind(NB - 1, 1, c)
                gate_and_count(NB - 2, c)
                if c == 11:
                    turn2(0, 0)
            turn2(1, 1)
            hidden2(0, 0)
            pe.wait_ge(run_done, NB - 1)
            for c in range(2 + KH):
                gate_and_count(NB - 1, c)

            pe.wait_ge(xl2_done, 1)
            turn2(2, 0)
            pe.wait_ge(gelu_done, NB * KH)
            hidden2(1, 1)

            def experts_of(i, n):
                _, es = nc.values_load_multi_w_load_instructions(
                    tab[0:1, 1, bass.ds(i * 2, 2 * n)], engines=[mybir.EngineType.PE], min_val=0, max_val=(E - 1) * 2 * D,
                    skip_runtime_bounds_check_because="the table holds min(e, E - 1) * 2 * D, e a sum of comparisons")
                return es

            def steps2(i, s, es, t_ok=True, h_ok=True):
                expert(i, s, es)
                if h_ok:
                    hidden2(i + 2, s)
                if t_ok:
                    pe.wait_ge(xl2_done, i + 2)
                    turn2(i + 3, 1 - s)

            def pass2(i, first=False, last=False):
                es = experts_of(i, PASS)
                for k in range(PASS):
                    if first and k == 1:
                        gate_and_count(NB - 1, 11)
                        pe.wait_ge(run_done, NB)
                    steps2(i + k, k % 2, es[2 * k:2 * k + 2], t_ok=not last or k + 3 < PASS,
                           h_ok=not last or k + 2 < PASS)

            pe.wait_ge(wdl_done, KH)
            pe.wait_ge(bdl_done, 1)
            pe.wait_ge(pick_in, 1)
            pe.wait_ge(early_done, 1)
            pass2(0, first=True)
            with pe.Fori(1, EARLY // 2 // PASS) as i:
                pass2(i * PASS)
            pe.wait_ge(tab_done, 1)
            with pe.Fori(EARLY // 2 // PASS, PAIRS // PASS - 1) as i:
                pass2(i * PASS)
            pass2(PAIRS - PASS, last=True)


def _constants():
    import numpy as np

    c = np.zeros((P, C_LEN), np.float32)
    c[:, C_ID:C_ID + P] = np.eye(P)
    c[:, C_TRI:C_TRI + P] = np.triu(np.ones((P, P)), 1)
    c[:, C_ONE:C_ONE + P] = 1
    c[:, C_IOTA:C_IOTA + E] = np.arange(E)
    c[:, C_BASE:C_BASE + E + 1] = np.arange(E + 1) * REGION
    c[:, C_HALF:C_HALF + BT] = -0.5
    c[:, C_E:C_E + BT * E] = np.e
    c[:, C_P] = np.arange(P)
    c[:, C_J:C_J + MAXT] = np.arange(MAXT)
    c[0, C_ROW0:C_ROW0 + P] = 1
    c[:, C_UPTO:C_UPTO + E * E] = np.tril(np.ones((E, E))).reshape(-1)
    c[:, C_MEAN:C_MEAN + BT] = 1 / D
    c[:, C_QUARTER:C_QUARTER + BT] = 0.25
    c[:, C_EPS:C_EPS + BT] = EPS
    tokens = np.arange(N, dtype=np.int32).reshape(N // P, P).T.copy()
    return c, tokens


def kernel(**inputs):
    import numpy as np
    import concourse.bacc as bacc
    from concourse.bass_utils import run_bass_kernel_spmd

    a = {k: np.asarray(v) for k, v in inputs.items()}
    consts, tokens = _constants()
    arrays = {
        "adj": a["adj"].reshape(NB, BN, NC, G, P).transpose(0, 2, 4, 3, 1).reshape(NB * NC * P, G * BN),
        "x": a["x"].reshape(NB, BT, P, D).transpose(0, 2, 1, 3).reshape(NB * P, BT * D),
        "w12": a["L0_gnn_weight"].reshape(2, D, D).transpose(1, 0, 2).reshape(D, 2 * D),
        "gnn_b": a["L0_gnn_bias"],
        "w1": a["L0_ffn_W1"],
        "b1": a["L0_ffn_b1"].reshape(KH, P).T,
        "wg": a["L0_ffn_Wg"].reshape(KH, P, E).transpose(1, 0, 2).reshape(P, KH * E),
        "bg": a["L0_ffn_bg"],
        "wd": a["L0_ffn_Wd"].reshape(E, KH, P, D).transpose(2, 1, 0, 3).reshape(P, KH * E * D),
        "bd": a["L0_ffn_bd"].reshape(E * D),
        "consts": consts,
        "tokens": tokens,
    }
    arrays = {k: np.ascontiguousarray(v) for k, v in arrays.items()}
    nc = bacc.Bacc("TRN2", target_bir_lowering=False, num_devices=1)
    args = [nc.dram_tensor(f"in_{k}", v.shape, mybir.dt.from_np(v.dtype), kind="ExternalInput").ap()
            for k, v in arrays.items()]
    order = ["x", "adj", "w12", "gnn_b", "w1", "b1", "wg", "bg", "wd", "bd", "consts", "tokens"]
    by = dict(zip(arrays, args))
    out = nc.dram_tensor("out", (N, D), F32, kind="ExternalOutput").ap()
    bass_gnn_moe_kernel(nc, *[by[k] for k in order], out)
    r = run_bass_kernel_spmd(nc, [{f"in_{k}": v for k, v in arrays.items()}], core_ids=[0])
    return r.results[0]["out"]
```
